# Optimizing a Trainium2 kernel written in Bass

```python
import numpy as np
import jax
import jax.numpy as jnp

def _softmax(x, axis=-1):
    return jax.nn.softmax(x, axis=axis)
def _gelu(x):
    return jax.nn.gelu(x, approximate=True)
def _silu(x):
    return jax.nn.silu(x)
def _sigmoid(x):
    return jax.nn.sigmoid(x)
def _layernorm(x, axis=-1, eps=1e-5):
    m = jnp.mean(x, axis=axis, keepdims=True)
    v = jnp.var(x, axis=axis, keepdims=True)
    return (x - m) / jnp.sqrt(v + eps)
def _scatter_add(tgt, idx, src, axis=0):
    return tgt.at[idx].add(src)
def _segment_sum(src, seg, n):
    return jax.ops.segment_sum(src, seg, n)

kernel_name = 'mk_conv_seq_d1_conv_nhwc512_e2e14b'

def setup_inputs(seed: int = 0):
    np.random.seed(seed)
    _w = jnp.asarray
    def _rec_inputs():
        import jax
        import jax.numpy as jnp
        _gk = jax.random.key(seed)
        x = 7.22e-05 + 1 * jax.random.normal(jax.random.fold_in(_gk, 1), (16, 32, 32, 512), jnp.float32)
        return x
    x = _rec_inputs()
    def _L0_conv_setup():
        import jax, jax.numpy as jnp
        import numpy as np
        GROUPS = 32
        EPS = 0.001

        def group_norm(x, gamma, beta):
            B, H, W, C = x.shape
            g = GROUPS
            xg = x.reshape(B, H, W, g, C // g)
            mean = jnp.mean(xg, axis=(1, 2, 4), keepdims=True)
            var = jnp.var(xg, axis=(1, 2, 4), keepdims=True)
            xn = (xg - mean) * jax.lax.rsqrt(var + EPS)
            xn = xn.reshape(B, H, W, C)
            return xn * gamma + beta
        key = jax.random.key(seed)
        ks = jax.random.split(key, 8)
        B, H, W, C = (16, 32, 32, 512)
        s = C ** (-0.5)
        return {'x': jax.random.normal(ks[0], (B, H, W, C), jnp.float32), 'gamma': jnp.ones((C,), jnp.float32), 'beta': jnp.zeros((C,), jnp.float32), 'wq': jax.random.normal(ks[1], (C, C), jnp.float32) * s, 'bq': jnp.zeros((C,), jnp.float32), 'wk': jax.random.normal(ks[2], (C, C), jnp.float32) * s, 'bk': jnp.zeros((C,), jnp.float32), 'wv': jax.random.normal(ks[3], (C, C), jnp.float32) * s, 'bv': jnp.zeros((C,), jnp.float32), 'wp': jax.random.normal(ks[4], (C, C), jnp.float32) * s, 'bp': jnp.zeros((C,), jnp.float32), 'index': 0}
    _L0_conv_all = _L0_conv_setup()
    _L0_conv_in = {k: v for k, v in _L0_conv_all.items() if k in ('gamma', 'beta', 'wq', 'bq', 'wk', 'bk', 'wv', 'bv', 'wp', 'bp', )}
    del _L0_conv_all

    return {
        "x": x,
        "L0_conv_gamma": _L0_conv_in["gamma"],
        "L0_conv_beta": _L0_conv_in["beta"],
        "L0_conv_wq": _L0_conv_in["wq"],
        "L0_conv_bq": _L0_conv_in["bq"],
        "L0_conv_wk": _L0_conv_in["wk"],
        "L0_conv_bk": _L0_conv_in["bk"],
        "L0_conv_wv": _L0_conv_in["wv"],
        "L0_conv_bv": _L0_conv_in["bv"],
        "L0_conv_wp": _L0_conv_in["wp"],
        "L0_conv_bp": _L0_conv_in["bp"],
    }

def reference(x, L0_conv_gamma, L0_conv_beta, L0_conv_wq, L0_conv_bq, L0_conv_wk, L0_conv_bk, L0_conv_wv, L0_conv_bv, L0_conv_wp, L0_conv_bp):
    import jax
    import jax.numpy as jnp
    def _L0_conv_ref(x, gamma, beta, wq, bq, wk, bk, wv, bv, wp, bp, index):
        import jax, jax.numpy as jnp
        import numpy as np
        GROUPS = 32
        EPS = 0.001

        def group_norm(x, gamma, beta):
            B, H, W, C = x.shape
            g = GROUPS
            xg = x.reshape(B, H, W, g, C // g)
            mean = jnp.mean(xg, axis=(1, 2, 4), keepdims=True)
            var = jnp.var(xg, axis=(1, 2, 4), keepdims=True)
            xn = (xg - mean) * jax.lax.rsqrt(var + EPS)
            xn = xn.reshape(B, H, W, C)
            return xn * gamma + beta
        B, H, W, C = x.shape
        N = H * W
        residual = x
        xn = group_norm(x, gamma, beta)
        xf = xn.reshape(B, N, C)
        q = xf @ wq + bq
        k = xf @ wk + bk
        v = xf @ wv + bv
        scores = jnp.einsum('bnc,bmc->bnm', q, k) * C ** (-0.5)
        attn = jax.nn.softmax(scores, axis=-1)
        out = jnp.einsum('bnm,bmc->bnc', attn, v)
        out = out @ wp + bp
        return out.reshape(B, H, W, C) + residual

    def _gn(v, G=32, eps=1e-5):
        B_, H_, W_, C_ = v.shape
        g = v.reshape(B_, H_, W_, G, C_ // G)
        m = jnp.mean(g, axis=(1, 2, 4), keepdims=True)
        s = jnp.var(g, axis=(1, 2, 4), keepdims=True)
        return ((g - m) / jnp.sqrt(s + eps)).reshape(v.shape)

    def _ln_c(v, eps=1e-6):
        m = jnp.mean(v, axis=-1, keepdims=True)
        s = jnp.var(v, axis=-1, keepdims=True)
        return (v - m) / jnp.sqrt(s + eps)

    def _ln_t(v, eps=1e-5):
        m = jnp.mean(v, axis=-1, keepdims=True)
        s = jnp.var(v, axis=-1, keepdims=True)
        return (v - m) / jnp.sqrt(s + eps)

    def _to_tokens(v):
        B_, H_, W_, C_ = v.shape
        return v.reshape(B_, H_ * W_, C_)
    def _from_tokens(t, like):
        return t.reshape(like.shape)

    x = _L0_conv_ref(x, L0_conv_gamma, L0_conv_beta, L0_conv_wq, L0_conv_bq, L0_conv_wk, L0_conv_bk, L0_conv_wv, L0_conv_bv, L0_conv_wp, L0_conv_bp, 0)
    return x


_drawn_inputs = setup_inputs


def setup_inputs(seed=0):
    import zlib

    import numpy as np

    out = dict(_drawn_inputs(seed))
    spreads = {'L0_conv_gamma': (1.0, 0.2),
     'L0_conv_beta': (0.0, 0.1),
     'L0_conv_bq': (0.0, 0.8),
     'L0_conv_bk': (0.0, 0.8),
     'L0_conv_bv': (0.0, 0.1),
     'L0_conv_bp': (0.0, 0.1)}
    factors = {}
    for name, (base, spread) in spreads.items():
        noise = np.random.default_rng([zlib.crc32(name.encode()), seed]).standard_normal(out[name].shape)
        drawn = base * np.exp(spread * noise) if base else spread * noise
        out[name] = jnp.asarray(drawn.astype(out[name].dtype))
    for name, factor in factors.items():
        out[name] = (out[name] * factor).astype(out[name].dtype)
    return out
```

```python
import concourse.bass as bass
from concourse import mybir
from contextlib import ExitStack

FP32 = mybir.dt.float32
F32R = mybir.dt.float32r
ALU = mybir.AluOpType
ACT = mybir.ActivationFunctionType
AX = mybir.AxisListType

P = 128
BANK = 512
GROUPS = 32
EPS = 0.001


def group_norm_attention(nc, x, gamma, beta, wq, bq, wk, bk, wv, bv, wp, bp, out):
    B, H, W, C = x.shape
    N = H * W
    KC = C // P
    NT = N // P
    NH = N // BANK
    TH = NT // NH
    PG = P // (C // GROUPS)
    CG = C // GROUPS
    SCALE = float(C) ** -0.5
    assert C == BANK and N == 2 * BANK and NT % 2 == 0

    x_rows = x.rearrange("b h w c -> b (h w) c").rearrange("b (t p) c -> b p t c", p=P)
    out_rows = out.rearrange("b h w c -> b (h w) c").rearrange("b (t p) c -> b p t c", p=P)

    ctx = ExitStack()
    with ctx:
        def sb(name, shape, dt=FP32, where=ctx):
            return where.enter_context(nc.sbuf_tensor(name, shape, dt))

        def sem(name):
            return ctx.enter_context(nc.semaphore(name))

        ident = sb("ident", [P, P])
        ones = sb("ones", [P, P])
        group_avg = sb("group_avg", [P, P])
        gamma_c = sb("gamma_c", [P, KC])
        beta_c = sb("beta_c", [P, KC])
        bq_c = sb("bq_c", [P, KC])
        bk_c = sb("bk_c", [P, KC])
        bv_c = sb("bv_c", [P, KC])
        bv_wide = sb("bv_wide", [P, KC, P])
        bp_row = sb("bp_row", [1, C])
        minus_half = sb("minus_half", [P, KC])
        wk_bq = sb("wk_bq", [P, KC])
        wq_bk = sb("wq_bk", [P, KC])
        bqbk_part = sb("bqbk_part", [P, 1])
        bqbk = sb("bqbk", [P, 1])
        out_bias = sb("out_bias", [P, C])

        x_in = sb("x_in", [P, NT, C])
        x_res = sb("x_res", [P, NT, C])
        x_t = sb("x_t", [P, KC, N])
        xn_hi = sb("xn_hi", [P, KC, N], F32R)
        xn_lo = sb("xn_lo", [P, KC, N], F32R)
        a_hi = sb("a_hi", [P, KC, C], F32R)
        a_lo = sb("a_lo", [P, KC, C], F32R)
        m_hi = sb("m_hi", [P, KC, C], F32R)
        m_lo = sb("m_lo", [P, KC, C], F32R)
        prob = sb("prob", [P, N])
        pt_hi = sb("pt_hi", [P, NT, P], F32R)
        pt_lo = sb("pt_lo", [P, NT, P], F32R)

        bn = sb("bn", [P, KC, NH, 6])
        mv = sb("mv", [P, KC, 2])
        g_mean = sb("g_mean", [P, KC])
        dev = sb("dev", [P, KC])
        g_var = sb("g_var", [P, KC])
        rstd = sb("rstd", [P, KC])
        scale_c = sb("scale_c", [P, KC])
        shift_c = sb("shift_c", [P, KC])
        row_w = sb("row_w", [P, KC])
        row_p = sb("row_p", [P, KC])
        row_s = sb("row_s", [P, 1])
        row_0 = sb("row_0", [P, 1])
        row_junk = sb("row_junk", [P, C])
        row_x = sb("row_x", [P, NT])
        row = sb("row", [P, NT])
        row_scaled = sb("row_scaled", [P, NT])
        top = sb("top", [P, NT])
        top_neg = sb("top_neg", [P, NT])
        exp_bias = sb("exp_bias", [P, NT])
        total = sb("total", [P, NT])
        total_inv = sb("total_inv", [P, NT])

        with ExitStack() as setup:
            w_q, w_k, w_v, w_p = (sb(n, [P, KC, C], where=setup) for n in ("w_q", "w_k", "w_v", "w_p"))
            wq_t, wk_t, wv_t = (sb(n, [P, KC, C], where=setup) for n in ("wq_t", "wk_t", "wv_t"))
        t_hi = sb("t_hi", [P, KC, N], F32R)
        t_lo = sb("t_lo", [P, KC, N], F32R)
        v_hi = sb("v_hi", [P, NT, C], F32R)
        v_lo = sb("v_lo", [P, NT, C], F32R)

        psum = ctx.enter_context(nc.psum_tensor("psum", [P, 8, BANK], FP32))
        scores = psum[:, 0:2, :].rearrange("p b n -> p (b n)")
        pt_ps = psum[:, 2:4, :]
        o_ps = psum[:, 4, :]
        work = [psum[:, 5, :], psum[:, 6, :]]
        stat = psum[:, 7, :]

        s_wload = [sem(f"w_loaded{i}") for i in range(4)]
        s_small = sem("small_loaded")
        s_const = sem("constants_made")
        s_set = sem("setup_product_done")
        s_setr = sem("setup_bank_read")
        s_setv = sem("setup_vector_step")
        s_x = [sem(f"x_half{h}_loaded") for h in range(NH)]
        s_res = sem("residual_ready")
        s_row = sem("row_terms_ready")
        s_work = sem("work_bank_full")
        s_free = sem("work_bank_read")
        s_hi = sem("hi_part_ready")
        s_stin = sem("stat_input_ready")
        s_stat = sem("stat_bank_full")
        s_sv = sem("stat_step")
        s_rv = sem("row_step")
        s_rp = sem("row_product_done")
        s_pw_in = sem("variance_ready")
        s_pw = sem("rstd_ready")
        s_norm = sem("chunk_normed")
        s_xh = sem("xn_hi_ready")
        s_xl = sem("xn_lo_ready")
        s_s = sem("scores_done")
        s_top = sem("top_ready")
        s_topn = sem("top_neg_ready")
        s_eb = sem("exp_bias_ready")
        s_p = sem("prob_ready")
        s_pt = sem("pt_bank_full")
        s_pth = sem("pt_hi_ready")
        s_ptl = sem("pt_lo_ready")
        s_o = sem("o_done")
        s_ti = sem("total_inv_ready")
        s_y = sem("out_tile_ready")
        s_st = [sem(f"out_tile{i}_stored") for i in range(NT)]

        block = ctx.enter_context(nc.Block())

        def use_x(n, i):
            return n * 3 * NT + i

        def use_t(n, c):
            return n * 3 * NT + NT + c

        def use_v(n, m):
            return n * 3 * NT + 2 * NT + m

        SET_T = 3 * KC
        SET_A = SET_T + 2 * KC
        SET_LAST = SET_A + 2

        STAT_STEPS = 7

        @block.sync
        def _(sp):
            for w, dst, s in ((wq, w_q, 0), (wk, w_k, 1)):
                sp.dma_start(dst[:], w.rearrange("(k p) n -> p k n", p=P)).then_inc(s_wload[s], 16)
            for h in range(NH):
                sp.dma_start(x_in[:, h * TH:(h + 1) * TH, :],
                             x_rows[0, :, h * TH:(h + 1) * TH, :]).then_inc(s_x[h], 16)
            for w, dst, s in ((wv, w_v, 2), (wp, w_p, 3)):
                sp.dma_start(dst[:], w.rearrange("(k p) n -> p k n", p=P)).then_inc(s_wload[s], 16)

            def image(b, more):
                if more:
                    sp.wait_ge(s_row, b + 1)
                    sp.wait_ge(s_res, b * NT + NT)
                    for h in range(NH):
                        sp.dma_start(x_in[:, h * TH:(h + 1) * TH, :],
                                     x_rows[b + 1, :, h * TH:(h + 1) * TH, :]).then_inc(s_x[h], 16)
                for i in range(NT):
                    sp.wait_ge(s_y, b * NT + i + 1)
                    sp.dma_start(out_rows[b, :, i, :], x_res[:, i, :]).then_inc(s_st[i], 16)

            if B > 1:
                with sp.Fori(0, B - 1) as b:
                    image(b, True)
            image(B - 1, False)
            for i in range(NT):
                sp.wait_ge(s_st[i], 16 * B)

        @block.gpsimd
        def _(pool):
            nc.gpsimd.memset(ones[:], 1.0).then_inc(s_const, 1)
            nc.gpsimd.memset(group_avg[:], 1.0 / CG).then_inc(s_const, 1)
            nc.gpsimd.memset(minus_half[:], -0.5).then_inc(s_const, 1)
            pool.wait_ge(s_const, 3)
            nc.gpsimd.affine_select(out=ident[:], in_=ones[:], compare_op=ALU.is_equal, fill=0.0, base=0,
                                    pattern=[[-1, P]], channel_multiplier=1).then_inc(s_const, 1)
            g = group_avg[:].rearrange("p (g c) -> p g c", c=CG)
            nc.gpsimd.affine_select(out=g, in_=g, compare_op=ALU.is_ge, fill=0.0, base=0,
                                    pattern=[[-CG, PG], [0, CG]], channel_multiplier=1).then_inc(s_const, 1)
            pool.wait_ge(s_const, 5)
            nc.gpsimd.affine_select(out=g, in_=g, compare_op=ALU.is_ge, fill=0.0, base=CG - 1,
                                    pattern=[[CG, PG], [0, CG]], channel_multiplier=-1).then_inc(s_const, 1)

            def root(n):
                pool.wait_ge(s_pw_in, n + 1)
                nc.gpsimd.tensor_tensor(rstd[:], g_var[:], minus_half[:], ALU.pow).then_inc(s_pw, 1)

            root(0)
            pool.wait_ge(s_setr, SET_LAST)

            def image(b, more):
                for i in range(NT):
                    pool.wait_ge(s_x[i // TH], b * 16 + 16)
                    pool.wait_ge(s_st[i], b * 16)
                    nc.gpsimd.tensor_tensor(x_res[:, i, :], x_in[:, i, :], out_bias[:],
                                            ALU.add).then_inc(s_res, 1)
                if more:
                    root(b + 1)

            if B > 1:
                with pool.Fori(0, B - 1) as b:
                    image(b, True)
            image(B - 1, False)

        @block.scalar
        def _(act):
            for src, dst in ((gamma, gamma_c), (beta, beta_c), (bq, bq_c), (bk, bk_c), (bv, bv_c)):
                act.dma_start(dst[:], src.rearrange("(k p) -> p k", p=P),
                              allow_slow_non_contiguous=True).then_inc(s_small, 16)
            act.dma_start(bp_row[:], bp.rearrange("(o c) -> o c", o=1)).then_inc(s_small, 16)

            def xn_split(n):
                for k in range(KC):
                    act.wait_ge(s_norm, n * KC + k + 1)
                    nc.scalar.activation(xn_hi[:, k, :], x_t[:, k, :], ACT.Copy).then_inc(s_xh, 1)

            def t_hi_part(n, c):
                h, j = c // KC, c % KC
                act.wait_ge(s_work, use_t(n, c) + 1)
                nc.scalar.activation(t_hi[:, j, h * BANK:(h + 1) * BANK], work[use_t(0, c) % 2], ACT.Identity,
                                     bias=wk_bq[:, j:j + 1]).then_inc(s_hi, 1)

            def pt_hi_part(b, i):
                for g in range(2):
                    act.wait_ge(s_pt, b * 2 * NT + 2 * i + g + 1)
                    nc.scalar.activation(pt_hi[:, g * KC:(g + 1) * KC, :].rearrange("p m n -> p (m n)"),
                                         pt_ps[:, g, :], ACT.Copy).then_inc(s_pth, 1)

            xn_split(0)
            act.wait_ge(s_setr, SET_A + 1)
            t_hi_part(0, 0)

            def image(b, more):
                for c in range(1, NT):
                    t_hi_part(b, c)
                for m in range(NT):
                    act.wait_ge(s_work, use_v(b, m) + 1)
                    nc.scalar.activation(v_hi[:, m, :], work[use_v(0, m) % 2], ACT.Copy).then_inc(s_hi, 1)
                for i in range(NT):
                    if i:
                        pt_hi_part(b, i - 1)
                    act.wait_ge(s_eb, b * NT + i + 1)
                    nc.scalar.activation(prob[:], scores, ACT.Exp, bias=exp_bias[:, i:i + 1], scale=SCALE,
                                         accum_out=total[:, i:i + 1]).then_inc(s_p, 1)
                if more:
                    xn_split(b + 1)
                pt_hi_part(b, NT - 1)
                if more:
                    t_hi_part(b + 1, 0)

            if B > 1:
                with act.Fori(0, B - 1) as b:
                    image(b, True)
            image(B - 1, False)

        @block.vector
        def _(dve):
            def lo_part(dst, src, hi, signal):
                nc.vector.tensor_tensor(dst, src, hi.bitcast(FP32), ALU.subtract).then_inc(signal, 1)

            for u in range(SET_T):
                dst = (wq_t, wk_t, wv_t)[u // KC]
                dve.wait_ge(s_set, u + 1)
                nc.vector.tensor_copy(dst[:, u % KC, :], psum[:, u % 4, :]).then_inc(s_setr, 1)
            dve.wait_ge(s_small, 16 * 6)
            dve.wait_ge(s_const, 6)
            for k in range(KC):
                nc.vector.tensor_scalar(bv_wide[:, k, :], ones[:], bv_c[:, k:k + 1], None, ALU.mult).then_inc(s_setv, 1)
            nc.vector.tensor_tensor(dev[:], bq_c[:], bk_c[:], ALU.mult).then_inc(s_setv, 1)
            dve.wait_ge(s_setv, KC + 1)
            nc.vector.reduce_sum(bqbk_part[:], dev[:], AX.X).then_inc(s_setv, 1)
            for u in range(2 * KC):
                hi, lo = (a_hi, a_lo) if u < KC else (m_hi, m_lo)
                bank = psum[:, (SET_T + u) % 4, :]
                dve.wait_ge(s_set, SET_T + u + 1)
                nc.vector.tensor_copy(hi[:, u % KC, :], bank).then_inc(s_setv, 1)
                dve.wait_ge(s_setv, KC + 3 + u)
                lo_part(lo[:, u % KC, :], bank, hi[:, u % KC, :], s_setr)
            dve.wait_ge(s_set, SET_A + 1)
            vec = psum[:, SET_A % 4, :]
            nc.vector.tensor_copy(wk_bq[:], vec[:, 0:KC]).then_inc(s_setv, 1)
            nc.vector.tensor_copy(wq_bk[:], vec[:, KC:2 * KC]).then_inc(s_setv, 1)
            nc.vector.tensor_copy(bqbk[:], vec[:, 2 * KC:2 * KC + 1]).then_inc(s_setr, 1)
            dve.wait_ge(s_set, SET_A + 2)
            nc.vector.tensor_copy(out_bias[:], psum[:, (SET_A + 1) % 4, :]).then_inc(s_setr, 1)

            def x_evict(n, i):
                dve.wait_ge(s_work, use_x(n, i) + 1)
                nc.vector.tensor_copy(x_t[:, :, i * P:(i + 1) * P],
                                      work[use_x(0, i) % 2].rearrange("p (k n) -> p k n", k=KC)).then_inc(s_free, 1)

            def half_stats(n, h):
                dve.wait_ge(s_free, use_x(n, (h + 1) * TH - 1) + 1)
                for k in range(KC):
                    last = nc.vector.bn_stats(bn[:, k, h, :], x_t[:, k, h * BANK:(h + 1) * BANK])
                last.then_inc(s_sv, 1)

            def channel_stats(n):
                for k in range(KC):
                    last = nc.vector.bn_aggr(mv[:, k, :], bn[:, k, :, :].rearrange("p h s -> p (h s)"))
                last.then_inc(s_stin, 1)

            def group_variance(n):
                dve.wait_ge(s_stin, n * 4 + 1)
                dve.wait_ge(s_stat, n * 4 + 1)
                nc.vector.tensor_copy(g_mean[:], stat[:, 0:KC])
                nc.vector.tensor_tensor(dev[:], mv[:, :, 0], stat[:, 0:KC], ALU.subtract).then_inc(s_sv, 1)
                dve.wait_ge(s_sv, n * STAT_STEPS + 3)
                nc.vector.tensor_tensor(dev[:], dev[:], dev[:], ALU.mult).then_inc(s_sv, 1)
                dve.wait_ge(s_sv, n * STAT_STEPS + 4)
                nc.vector.tensor_tensor(dev[:], dev[:], mv[:, :, 1], ALU.add).then_inc(s_stin, 1)

            def norm(n):
                dve.wait_ge(s_stat, n * 4 + 2)
                nc.vector.tensor_scalar(g_var[:], stat[:, 0:KC], EPS, None, ALU.add).then_inc(s_pw_in, 1)
                dve.wait_ge(s_pw, n + 1)
                nc.vector.tensor_tensor(scale_c[:], rstd[:], gamma_c[:], ALU.mult).then_inc(s_sv, 1)
                dve.wait_ge(s_sv, n * STAT_STEPS + 5)
                nc.vector.tensor_tensor(dev[:], g_mean[:], scale_c[:], ALU.mult).then_inc(s_sv, 1)
                dve.wait_ge(s_sv, n * STAT_STEPS + 6)
                nc.vector.tensor_tensor(shift_c[:], beta_c[:], dev[:], ALU.subtract).then_inc(s_sv, 1)
                dve.wait_ge(s_sv, n * STAT_STEPS + 7)
                for k in range(KC):
                    nc.vector.tensor_scalar(x_t[:, k, :], x_t[:, k, :], scale_c[:, k:k + 1], shift_c[:, k:k + 1],
                                            ALU.mult, ALU.add).then_inc(s_norm, 1)

            def xn_lo_parts(n):
                for k in range(KC):
                    dve.wait_ge(s_xh, n * KC + k + 1)
                    lo_part(xn_lo[:, k, :], x_t[:, k, :], xn_hi[:, k, :], s_xl)

            def t_lo_part(n, c):
                h, j = c // KC, c % KC
                dve.wait_ge(s_hi, n * 2 * NT + c + 1)
                at = (slice(None), j, slice(h * BANK, (h + 1) * BANK))
                nc.vector.scalar_tensor_tensor(out=t_lo[at], in0=work[use_t(0, c) % 2], scalar=wk_bq[:, j:j + 1],
                                               in1=t_hi[at].bitcast(FP32), op0=ALU.add,
                                               op1=ALU.subtract).then_inc(s_free, 1)

            ROW_STEPS = 3

            def row_sums(n):
                nc.vector.tensor_tensor(row_w[:], scale_c[:], wq_bk[:], ALU.mult).then_inc(s_rv, 1)
                nc.vector.tensor_tensor(row_p[:], shift_c[:], wq_bk[:], ALU.mult).then_inc(s_rv, 1)
                dve.wait_ge(s_rv, n * ROW_STEPS + 2)
                nc.vector.reduce_sum(row_s[:], row_p[:], AX.X).then_inc(s_stin, 1)

            def row_spread(n):
                dve.wait_ge(s_stat, n * 4 + 3)
                nc.vector.tensor_tensor(row_0[:], bqbk[:], stat[:, 0:1], ALU.add)
                for k in range(KC):
                    last = nc.vector.tensor_scalar(row_junk[:, k * P:(k + 1) * P], ident[:], row_w[:, k:k + 1],
                                                   None, ALU.mult)
                last.then_inc(s_stin, 1)

            def row_terms(n):
                dve.wait_ge(s_stat, n * 4 + 4)
                for i in range(NT):
                    dve.wait_ge(s_rp, n * NT + i)
                    nc.vector.tensor_tensor_reduce(out=row_junk[:], in0=x_in[:, i, :], in1=stat, scale=1.0,
                                                   scalar=0.0, op0=ALU.mult, op1=ALU.add,
                                                   accum_out=row_x[:, i:i + 1]).then_inc(s_rp, 1)
                dve.wait_ge(s_rp, n * NT + NT)
                nc.vector.tensor_scalar(row[:], row_x[:], row_0[:], None, ALU.add).then_inc(s_rv, 1)
                dve.wait_ge(s_rv, n * ROW_STEPS + 3)
                nc.vector.tensor_scalar(row_scaled[:], row[:], SCALE, None, ALU.mult).then_inc(s_row, 1)

            def pt_lo_part(b, i):
                for g in range(2):
                    dve.wait_ge(s_pth, b * 2 * NT + 2 * i + g + 1)
                    part = slice(g * KC, (g + 1) * KC)
                    lo_part(pt_lo[:, part, :].rearrange("p m n -> p (m n)"), pt_ps[:, g, :],
                            pt_hi[:, part, :].rearrange("p m n -> p (m n)"), s_ptl)

            def tile_top(b, i):
                dve.wait_ge(s_s, b * NT + i + 1)
                nc.vector.reduce_max(top[:, i:i + 1], scores, AX.X).then_inc(s_top, 1)
                dve.wait_ge(s_top, b * NT + i + 1)
                nc.vector.tensor_scalar(top_neg[:, i:i + 1], top[:, i:i + 1], row[:, i:i + 1], -SCALE,
                                        ALU.add, ALU.mult).then_inc(s_topn, 1)
                dve.wait_ge(s_topn, b * NT + i + 1)
                nc.vector.tensor_scalar(exp_bias[:, i:i + 1], top_neg[:, i:i + 1], row_scaled[:, i:i + 1], None,
                                        ALU.add).then_inc(s_eb, 1)

            def tile_out(b, i):
                dve.wait_ge(s_p, b * NT + i + 1)
                nc.vector.reciprocal(total_inv[:, i:i + 1], total[:, i:i + 1]).then_inc(s_ti, 1)
                dve.wait_ge(s_o, b * NT + i + 1)
                dve.wait_ge(s_res, b * NT + i + 1)
                dve.wait_ge(s_ti, b * NT + i + 1)
                nc.vector.scalar_tensor_tensor(out=x_res[:, i, :], in0=o_ps, scalar=total_inv[:, i:i + 1],
                                               in1=x_res[:, i, :], op0=ALU.mult, op1=ALU.add).then_inc(s_y, 1)

            for i in range(NT):
                x_evict(0, i)
            half_stats(0, 0)
            half_stats(0, 1)
            dve.wait_ge(s_sv, NH)
            channel_stats(0)
            group_variance(0)
            norm(0)
            xn_lo_parts(0)
            t_lo_part(0, 0)

            def image(b, more):
                row_sums(b)
                for c in range(1, NT):
                    t_lo_part(b, c)
                    if c == 1:
                        row_spread(b)
                for m in range(NT):
                    dve.wait_ge(s_hi, b * 2 * NT + NT + m + 1)
                    lo_part(v_lo[:, m, :], work[use_v(0, m) % 2], v_hi[:, m, :], s_free)
                    if m == 0:
                        row_terms(b)
                for i in range(NT):
                    if more and i == 5:
                        dve.wait_ge(s_sv, (b + 1) * STAT_STEPS + NH)
                    if i >= 2:
                        tile_out(b, i - 2)
                    if more and i == 5:
                        channel_stats(b + 1)
                    if i >= 1:
                        pt_lo_part(b, i - 1)
                    tile_top(b, i)
                    if more:
                        if i < NT // 2:
                            x_evict(b + 1, 2 * i)
                            x_evict(b + 1, 2 * i + 1)
                        if i == 1:
                            half_stats(b + 1, 0)
                        if i == 4:
                            half_stats(b + 1, 1)
                        if i == 5:
                            group_variance(b + 1)
                        if i == 6:
                            norm(b + 1)
                if more:
                    xn_lo_parts(b + 1)
                tile_out(b, NT - 2)
                pt_lo_part(b, NT - 1)
                if more:
                    t_lo_part(b + 1, 0)
                tile_out(b, NT - 1)

            if B > 1:
                with dve.Fori(0, B - 1) as b:
                    image(b, True)
            image(B - 1, False)

        @block.tensor
        def _(pe):
            def product(dst, pairs):
                for n, (s_hi_, s_lo_, m_hi_, m_lo_) in enumerate(pairs):
                    nc.tensor.matmul(dst, s_hi_, m_hi_, start=n == 0, stop=False)
                    nc.tensor.matmul(dst, s_hi_, m_lo_, start=False, stop=False)
                    last = nc.tensor.matmul(dst, s_lo_, m_hi_, start=False, stop=n == len(pairs) - 1)
                return last

            def chunk(c):
                return slice(c * P, (c + 1) * P)

            def setup_bank(u):
                if u >= 4:
                    pe.wait_ge(s_setr, u - 3)
                return psum[:, u % 4, :]

            pe.wait_ge(s_const, 6)
            u = 0
            for s, w in ((0, w_q), (1, w_k), (2, w_v)):
                pe.wait_ge(s_wload[s], 16)
                for j in range(KC):
                    bank = setup_bank(u)
                    for k in range(KC):
                        last = nc.tensor.transpose(bank[:, chunk(k)], w[:, k, chunk(j)], ident[:])
                    last.then_inc(s_set, 1)
                    u += 1
            for left, right in ((wq_t, wk_t), (wv_t, w_p)):
                if right is w_p:
                    pe.wait_ge(s_wload[3], 16)
                for k in range(KC):
                    bank = setup_bank(u)
                    if u == SET_T:
                        pe.wait_ge(s_setr, SET_T)
                    for j in range(KC):
                        last = nc.tensor.matmul(bank, left[:, j, chunk(k)], right[:, j, :],
                                                start=j == 0, stop=j == KC - 1)
                    last.then_inc(s_set, 1)
                    u += 1
            bank = setup_bank(u)
            pe.wait_ge(s_setv, KC + 2)
            for n, (w_t, vec) in enumerate(((wk_t, bq_c), (wq_t, bk_c))):
                for k in range(KC):
                    for j in range(KC):
                        nc.tensor.matmul(bank[:, n * KC + k:n * KC + k + 1], w_t[:, j, chunk(k)], vec[:, j:j + 1],
                                         start=j == 0, stop=j == KC - 1)
            nc.tensor.matmul(bank[:, 2 * KC:2 * KC + 1], ones[:], bqbk_part[:], start=True, stop=True).then_inc(s_set, 1)
            u += 1
            bank = setup_bank(u)
            for j in range(KC):
                nc.tensor.matmul(bank, bv_wide[:, j, :], w_p[:, j, :], start=j == 0, stop=False)
            nc.tensor.matmul(bank, ones[0:1, :], bp_row[:], start=False, stop=True).then_inc(s_set, 1)

            def work_bank(use, parity):
                pe.wait_ge(s_free, use - 1)
                return work[parity % 2]

            def x_transpose(n, i):
                use = use_x(n, i)
                if i % TH == 0:
                    pe.wait_ge(s_x[i // TH], n * 16 + 16)
                bank = work[i % 2] if isinstance(n, int) and n == 0 and i < 2 else work_bank(use, i)
                for k in range(KC):
                    last = nc.tensor.transpose(bank[:, chunk(k)], x_in[:, i, chunk(k)], ident[:])
                last.then_inc(s_work, 1)

            def group_sum(n, step, rhs):
                pe.wait_ge(s_stin, n * 4 + step + 1)
                nc.tensor.matmul(stat[:, 0:KC], group_avg[:], rhs, start=True, stop=True).then_inc(s_stat, 1)

            def t_chunk(n, c):
                h, j = c // KC, c % KC
                tokens = slice(h * BANK, (h + 1) * BANK)
                dst = work_bank(use_t(n, c), use_t(0, c))
                if c == 0:
                    pe.wait_ge(s_xl, n * KC + KC)
                product(dst, [(a_hi[:, k, chunk(j)], a_lo[:, k, chunk(j)], xn_hi[:, k, tokens], xn_lo[:, k, tokens])
                              for k in range(KC)]).then_inc(s_work, 1)

            def v_tile(n, m):
                dst = work_bank(use_v(n, m), use_v(0, m))
                product(dst, [(xn_hi[:, k, chunk(m)], xn_lo[:, k, chunk(m)], m_hi[:, k, :], m_lo[:, k, :])
                              for k in range(KC)]).then_inc(s_work, 1)

            def score_tile(b, i):
                if i == 0:
                    pe.wait_ge(s_free, use_v(b, 0))
                for h in range(NH):
                    tokens = slice(h * BANK, (h + 1) * BANK)
                    last = product(scores[:, tokens], [(t_hi[:, k, chunk(i)], t_lo[:, k, chunk(i)],
                                                        xn_hi[:, k, tokens], xn_lo[:, k, tokens]) for k in range(KC)])
                last.then_inc(s_s, 1)

            def prob_transpose(b, i):
                pe.wait_ge(s_p, b * NT + i + 1)
                for m in range(NT):
                    last = nc.tensor.transpose(pt_ps[:, m // KC, chunk(m % KC)], prob[:, chunk(m)], ident[:])
                    if m % KC == KC - 1:
                        last.then_inc(s_pt, 1)

            def out_tile(b, i):
                if i == 0:
                    pe.wait_ge(s_free, use_v(b, NT - 1) + 1)
                pe.wait_ge(s_y, b * NT + i)
                for m in range(NT):
                    if m % KC == 0:
                        pe.wait_ge(s_ptl, b * 2 * NT + 2 * i + m // KC + 1)
                    nc.tensor.matmul(o_ps, pt_hi[:, m, :], v_hi[:, m, :], start=m == 0, stop=False)
                    nc.tensor.matmul(o_ps, pt_hi[:, m, :], v_lo[:, m, :], start=False, stop=False)
                    last = nc.tensor.matmul(o_ps, pt_lo[:, m, :], v_hi[:, m, :], start=False, stop=m == NT - 1)
                last.then_inc(s_o, 1)

            for i in range(NT):
                x_transpose(0, i)
            group_sum(0, 0, mv[:, :, 0])
            group_sum(0, 1, dev[:])
            t_chunk(0, 0)

            def image(b, more):
                for c in range(1, NT):
                    t_chunk(b, c)
                    if c == 1:
                        pe.wait_ge(s_stin, b * 4 + 3)
                        nc.tensor.matmul(stat[:, 0:1], ones[:], row_s[:], start=True, stop=True).then_inc(s_stat, 1)
                    if c == 4:
                        pe.wait_ge(s_stin, b * 4 + 4)
                        nc.tensor.matmul(stat, ones[:], row_junk[:], start=True, stop=True).then_inc(s_stat, 1)
                for m in range(NT):
                    v_tile(b, m)
                for i in range(NT):
                    if i >= 1:
                        prob_transpose(b, i - 1)
                    score_tile(b, i)
                    if more:
                        if i < NT // 2:
                            x_transpose(b + 1, 2 * i)
                            x_transpose(b + 1, 2 * i + 1)
                        if i == 5:
                            group_sum(b + 1, 0, mv[:, :, 0])
                        if i == 6:
                            group_sum(b + 1, 1, dev[:])
                    if i >= 1:
                        out_tile(b, i - 1)
                prob_transpose(b, NT - 1)
                if more:
                    t_chunk(b + 1, 0)
                out_tile(b, NT - 1)

            if B > 1:
                with pe.Fori(0, B - 1) as b:
                    image(b, True)
            image(B - 1, False)


_INS = ["x"] + ["L0_conv_" + n for n in ("gamma", "beta", "wq", "bq", "wk", "bk", "wv", "bv", "wp", "bp")]


def kernel(**inputs):
    import numpy as _np
    import concourse.bacc as _bacc
    from concourse.bass_utils import run_bass_kernel_spmd as _run

    nc = _bacc.Bacc("TRN2", target_bir_lowering=False, num_devices=1)
    arrays, args = {}, []
    for name in _INS:
        a = _np.ascontiguousarray(inputs[name])
        arrays[f"in_{name}_dram"] = a
        args.append(nc.dram_tensor(f"in_{name}_dram", a.shape, mybir.dt.from_np(a.dtype), kind="ExternalInput").ap())
    args.append(nc.dram_tensor("out_dram", inputs["x"].shape, FP32, kind="ExternalOutput").ap())
    group_norm_attention(nc, *args)
    r = _run(nc, [arrays], core_ids=[0])
    return r.results[0]["out_dram"]
```

```python
import concourse.bass as bass
from concourse import mybir
from contextlib import ExitStack

FP32 = mybir.dt.float32
F32R = mybir.dt.float32r
ALU = mybir.AluOpType
ACT = mybir.ActivationFunctionType
AX = mybir.AxisListType

P = 128
BANK = 512
GROUPS = 32
EPS = 0.001


def group_norm_attention(nc, x, gamma, beta, wq, bq, wk, bk, wv, bv, wp, bp, out):
    B, H, W, C = x.shape
    N = H * W
    KC = C // P
    NT = N // P
    NH = N // BANK
    TH = NT // NH
    PG = P // (C // GROUPS)
    CG = C // GROUPS
    SCALE = float(C) ** -0.5
    assert C == BANK and N == 2 * BANK and NT % 2 == 0

    x_rows = x.rearrange("b h w c -> b (h w) c").rearrange("b (t p) c -> b p t c", p=P)
    out_rows = out.rearrange("b h w c -> b (h w) c").rearrange("b (t p) c -> b p t c", p=P)

    ctx = ExitStack()
    with ctx:
        def sb(name, shape, dt=FP32, where=ctx):
            return where.enter_context(nc.sbuf_tensor(name, shape, dt))

        def sem(name):
            return ctx.enter_context(nc.semaphore(name))

        ident = sb("ident", [P, P])
        ones = sb("ones", [P, P])
        group_avg = sb("group_avg", [P, P])
        vec_rows = sb("vec_rows", [5 * KC, P])
        vec_cols = sb("vec_cols", [P, 5 * KC])
        gamma_c, beta_c, bq_c, bk_c, bv_c = (vec_cols[:, n * KC:(n + 1) * KC] for n in range(5))
        bv_wide = sb("bv_wide", [P, KC, P])
        bp_row = sb("bp_row", [1, C])
        minus_half = sb("minus_half", [P, KC])
        wk_bq = sb("wk_bq", [P, KC])
        wq_bk = sb("wq_bk", [P, KC])
        bqbk_part = sb("bqbk_part", [P, 1])
        bqbk = sb("bqbk", [P, 1])
        out_bias = sb("out_bias", [P, C])

        x_in = sb("x_in", [P, NT, C])
        x_res = sb("x_res", [P, NT, C])
        x_t = sb("x_t", [P, KC, N])
        xn_hi = sb("xn_hi", [P, KC, N], F32R)
        xn_lo = sb("xn_lo", [P, KC, N], F32R)
        a_hi = sb("a_hi", [P, KC, C], F32R)
        a_lo = sb("a_lo", [P, KC, C], F32R)
        m_hi = sb("m_hi", [P, KC, C], F32R)
        m_lo = sb("m_lo", [P, KC, C], F32R)
        prob = sb("prob", [P, N])
        pt_hi = sb("pt_hi", [P, NT, P], F32R)
        pt_lo = sb("pt_lo", [P, NT, P], F32R)

        bn = sb("bn", [P, KC, NH, 6])
        mv = sb("mv", [P, KC, 2])
        g_mean = sb("g_mean", [P, KC])
        dev = sb("dev", [P, KC])
        bq_bk = sb("bq_times_bk", [P, KC])
        g_var = sb("g_var", [P, KC])
        rstd = sb("rstd", [P, KC])
        scale_c = sb("scale_c", [P, KC])
        shift_c = sb("shift_c", [P, KC])
        row_w = sb("row_w", [P, KC])
        row_p = sb("row_p", [P, KC])
        row_s = sb("row_s", [P, 1])
        row_0 = sb("row_0", [P, 1])
        row_junk = sb("row_junk", [P, C])
        row_x = sb("row_x", [P, NT])
        row = sb("row", [P, NT])
        row_scaled = sb("row_scaled", [P, NT])
        top = sb("top", [P, NT])
        top_neg = sb("top_neg", [P, NT])
        exp_bias = sb("exp_bias", [P, NT])
        total = sb("total", [P, NT])
        total_inv = sb("total_inv", [P, NT])

        with ExitStack() as setup:
            w_q, w_k, w_v, w_p = (sb(n, [P, KC, C], where=setup) for n in ("w_q", "w_k", "w_v", "w_p"))
            wq_t, wk_t, wv_t = (sb(n, [P, KC, C], where=setup) for n in ("wq_t", "wk_t", "wv_t"))
        t_hi = sb("t_hi", [P, KC, N], F32R)
        t_lo = sb("t_lo", [P, KC, N], F32R)
        v_hi = sb("v_hi", [P, NT, C], F32R)
        v_lo = sb("v_lo", [P, NT, C], F32R)

        psum = ctx.enter_context(nc.psum_tensor("psum", [P, 8, BANK], FP32))
        scores = psum[:, 0:2, :].rearrange("p b n -> p (b n)")
        pt_ps = psum[:, 2:4, :]
        o_ps = psum[:, 4, :]
        work = [psum[:, 5, :], psum[:, 6, :]]
        stat = psum[:, 7, :]

        s_wload = [sem(f"w_loaded{i}") for i in range(4)]
        s_small = sem("small_loaded")
        s_vec = sem("vectors_transposed")
        s_const = sem("constants_made")
        s_set = sem("setup_product_done")
        s_wt = sem("setup_weight_read")
        s_seth = sem("setup_hi_ready")
        s_setr = sem("setup_bank_read")
        s_setv = sem("setup_vector_step")
        s_x = [sem(f"x_half{h}_loaded") for h in range(NH)]
        s_res = sem("residual_ready")
        s_row = sem("row_terms_ready")
        s_work = sem("work_bank_full")
        s_free = sem("work_bank_read")
        s_hi = sem("hi_part_ready")
        s_stin = sem("stat_input_ready")
        s_stat = sem("stat_bank_full")
        s_sv = sem("stat_step")
        s_rv = sem("row_step")
        s_rp = sem("row_product_done")
        s_pw_in = sem("variance_ready")
        s_pw = sem("rstd_ready")
        s_norm = sem("chunk_normed")
        s_xh = sem("xn_hi_ready")
        s_xl = sem("xn_lo_ready")
        s_s = sem("scores_done")
        s_top = sem("top_ready")
        s_topn = sem("top_neg_ready")
        s_eb = sem("exp_bias_ready")
        s_p = sem("prob_ready")
        s_pt = sem("pt_bank_full")
        s_pth = sem("pt_hi_ready")
        s_ptl = sem("pt_lo_ready")
        s_o = sem("o_done")
        s_ti = sem("total_inv_ready")
        s_y = sem("out_tile_ready")
        s_st = [sem(f"out_tile{i}_stored") for i in range(NT)]

        block = ctx.enter_context(nc.Block())

        def use_x(n, i):
            return n * 3 * NT + i

        def use_t(n, c):
            return n * 3 * NT + NT + c

        def use_v(n, m):
            return n * 3 * NT + 2 * NT + m

        SET_WQ, SET_WK, SET_A, SET_WV, SET_M, SET_VEC, SET_BIAS = (0, KC, 2 * KC, 3 * KC, 4 * KC, 5 * KC, 5 * KC + 1)

        def weight_use(u):
            return u < SET_A or SET_WV <= u < SET_M

        def reads(u):
            return sum(weight_use(v) == weight_use(u) for v in range(u + 1))

        STAT_STEPS = 7

        @block.sync
        def _(sp):
            for h in range(NH):
                sp.dma_start(x_in[:, h * TH:(h + 1) * TH, :],
                             x_rows[0, :, h * TH:(h + 1) * TH, :]).then_inc(s_x[h], 16)
            for w, dst, s in ((wq, w_q, 0), (wk, w_k, 1), (wv, w_v, 2), (wp, w_p, 3)):
                sp.dma_start(dst[:], w.rearrange("(k p) n -> p k n", p=P)).then_inc(s_wload[s], 16)

            def image(b, more):
                if more:
                    sp.wait_ge(s_row, b + 1)
                    sp.wait_ge(s_res, b * NT + NT)
                    for h in range(NH):
                        sp.dma_start(x_in[:, h * TH:(h + 1) * TH, :],
                                     x_rows[b + 1, :, h * TH:(h + 1) * TH, :]).then_inc(s_x[h], 16)
                for i in range(NT):
                    sp.wait_ge(s_y, b * NT + i + 1)
                    sp.dma_start(out_rows[b, :, i, :], x_res[:, i, :]).then_inc(s_st[i], 16)

            if B > 1:
                with sp.Fori(0, B - 1) as b:
                    image(b, True)
            image(B - 1, False)
            for i in range(NT):
                sp.wait_ge(s_st[i], 16 * B)

        @block.gpsimd
        def _(pool):
            nc.gpsimd.memset(ones[:], 1.0).then_inc(s_const, 1)
            nc.gpsimd.memset(group_avg[:], 1.0 / CG).then_inc(s_const, 1)
            nc.gpsimd.memset(minus_half[:], -0.5).then_inc(s_const, 1)
            pool.wait_ge(s_const, 3)
            nc.gpsimd.affine_select(out=ident[:], in_=ones[:], compare_op=ALU.is_equal, fill=0.0, base=0,
                                    pattern=[[-1, P]], channel_multiplier=1).then_inc(s_const, 1)
            g = group_avg[:].rearrange("p (g c) -> p g c", c=CG)
            nc.gpsimd.affine_select(out=g, in_=g, compare_op=ALU.is_ge, fill=0.0, base=0,
                                    pattern=[[-CG, PG], [0, CG]], channel_multiplier=1).then_inc(s_const, 1)
            pool.wait_ge(s_const, 5)
            nc.gpsimd.affine_select(out=g, in_=g, compare_op=ALU.is_ge, fill=0.0, base=CG - 1,
                                    pattern=[[CG, PG], [0, CG]], channel_multiplier=-1).then_inc(s_const, 1)

            def root(n):
                pool.wait_ge(s_pw_in, n + 1)
                nc.gpsimd.tensor_tensor(rstd[:], g_var[:], minus_half[:], ALU.pow).then_inc(s_pw, 1)

            root(0)
            pool.wait_ge(s_setr, reads(SET_BIAS))

            def image(b, more):
                for i in range(NT):
                    pool.wait_ge(s_x[i // TH], b * 16 + 16)
                    pool.wait_ge(s_st[i], b * 16)
                    nc.gpsimd.tensor_tensor(x_res[:, i, :], x_in[:, i, :], out_bias[:],
                                            ALU.add).then_inc(s_res, 1)
                if more:
                    root(b + 1)

            if B > 1:
                with pool.Fori(0, B - 1) as b:
                    image(b, True)
            image(B - 1, False)

        @block.scalar
        def _(act):
            for n, vec in enumerate((gamma, beta, bq, bk, bv)):
                act.dma_start(vec_rows[n * KC:(n + 1) * KC, :], vec.rearrange("(k p) -> k p", p=P)).then_inc(s_small, 16)
            act.dma_start(bp_row[:], bp.rearrange("(o c) -> o c", o=1)).then_inc(s_small, 16)

            def tile_exp(b, i):
                act.wait_ge(s_eb, b * NT + i + 1)
                nc.scalar.activation(prob[:], scores, ACT.Exp, bias=exp_bias[:, i:i + 1], scale=SCALE,
                                     accum_out=total[:, i:i + 1]).then_inc(s_p, 1)

            def xn_split(n, first=0, end=KC):
                for k in range(first, end):
                    act.wait_ge(s_norm, n * KC + k + 1)
                    nc.scalar.activation(xn_hi[:, k, :], x_t[:, k, :], ACT.Copy).then_inc(s_xh, 1)

            def t_hi_part(n, c):
                h, j = c // KC, c % KC
                act.wait_ge(s_work, use_t(n, c) + 1)
                nc.scalar.activation(t_hi[:, j, h * BANK:(h + 1) * BANK], work[use_t(0, c) % 2], ACT.Identity,
                                     bias=wk_bq[:, j:j + 1]).then_inc(s_hi, 1)

            def pt_hi_part(b, i):
                for g in range(2):
                    act.wait_ge(s_pt, b * 2 * NT + 2 * i + g + 1)
                    nc.scalar.activation(pt_hi[:, g * KC:(g + 1) * KC, :].rearrange("p m n -> p (m n)"),
                                         pt_ps[:, g, :], ACT.Copy).then_inc(s_pth, 1)

            def weight_copies(u0, dst):
                for j in range(KC):
                    act.wait_ge(s_set, u0 + j + 1)
                    nc.scalar.activation(dst[:, j, :], psum[:, (u0 + j) % 4, :], ACT.Copy).then_inc(s_wt, 1)

            def setup_hi_parts(u0, dst):
                for k in range(KC):
                    act.wait_ge(s_set, u0 + k + 1)
                    nc.scalar.activation(dst[:, k, :], psum[:, (u0 + k) % 4, :], ACT.Copy).then_inc(s_seth, 1)

            weight_copies(SET_WQ, wq_t)
            weight_copies(SET_WK, wk_t)
            setup_hi_parts(SET_A, a_hi)
            weight_copies(SET_WV, wv_t)
            xn_split(0)
            setup_hi_parts(SET_M, m_hi)
            act.wait_ge(s_setr, reads(SET_VEC))
            t_hi_part(0, 0)

            def image(b, more):
                for c in range(1, NT):
                    t_hi_part(b, c)
                for m in range(NT):
                    if m == NT - 1:
                        tile_exp(b, 0)
                    act.wait_ge(s_work, use_v(b, m) + 1)
                    nc.scalar.activation(v_hi[:, m, :], work[use_v(0, m) % 2], ACT.Copy).then_inc(s_hi, 1)
                for i in range(1, NT):
                    pt_hi_part(b, i - 1)
                    if i == NT - 1 and more:
                        act.wait_ge(s_s, b * NT + NT)
                        xn_split(b + 1, 0, 2)
                    tile_exp(b, i)
                if more:
                    xn_split(b + 1, 2, KC)
                pt_hi_part(b, NT - 1)
                if more:
                    t_hi_part(b + 1, 0)

            if B > 1:
                with act.Fori(0, B - 1) as b:
                    image(b, True)
            image(B - 1, False)

        @block.vector
        def _(dve):
            def lo_part(dst, src, hi, signal):
                nc.vector.tensor_tensor(dst, src, hi.bitcast(FP32), ALU.subtract).then_inc(signal, 1)

            def x_evict(n, i):
                dve.wait_ge(s_work, use_x(n, i) + 1)
                nc.vector.tensor_copy(x_t[:, :, i * P:(i + 1) * P],
                                      work[use_x(0, i) % 2].rearrange("p (k n) -> p k n", k=KC)).then_inc(s_free, 1)

            def half_stats(n, h):
                dve.wait_ge(s_free, use_x(n, (h + 1) * TH - 1) + 1)
                for k in range(KC):
                    last = nc.vector.bn_stats(bn[:, k, h, :], x_t[:, k, h * BANK:(h + 1) * BANK])
                last.then_inc(s_sv, 1)

            def channel_stats(n):
                for k in range(KC):
                    last = nc.vector.bn_aggr(mv[:, k, :], bn[:, k, :, :].rearrange("p h s -> p (h s)"))
                last.then_inc(s_stin, 1)

            def group_variance(n):
                dve.wait_ge(s_stin, n * 4 + 1)
                dve.wait_ge(s_stat, n * 4 + 1)
                nc.vector.tensor_copy(g_mean[:], stat[:, 0:KC])
                nc.vector.tensor_tensor(dev[:], mv[:, :, 0], stat[:, 0:KC], ALU.subtract).then_inc(s_sv, 1)
                dve.wait_ge(s_sv, n * STAT_STEPS + 3)
                nc.vector.tensor_tensor(dev[:], dev[:], dev[:], ALU.mult).then_inc(s_sv, 1)
                dve.wait_ge(s_sv, n * STAT_STEPS + 4)
                nc.vector.tensor_tensor(dev[:], dev[:], mv[:, :, 1], ALU.add).then_inc(s_stin, 1)

            def norm(n):
                dve.wait_ge(s_stat, n * 4 + 2)
                nc.vector.tensor_scalar(g_var[:], stat[:, 0:KC], EPS, None, ALU.add).then_inc(s_pw_in, 1)
                dve.wait_ge(s_pw, n + 1)
                nc.vector.tensor_tensor(scale_c[:], rstd[:], gamma_c, ALU.mult).then_inc(s_sv, 1)
                dve.wait_ge(s_sv, n * STAT_STEPS + 5)
                nc.vector.tensor_tensor(dev[:], g_mean[:], scale_c[:], ALU.mult).then_inc(s_sv, 1)
                dve.wait_ge(s_sv, n * STAT_STEPS + 6)
                nc.vector.tensor_tensor(shift_c[:], beta_c, dev[:], ALU.subtract).then_inc(s_sv, 1)
                dve.wait_ge(s_sv, n * STAT_STEPS + 7)
                for k in range(KC):
                    nc.vector.tensor_scalar(x_t[:, k, :], x_t[:, k, :], scale_c[:, k:k + 1], shift_c[:, k:k + 1],
                                            ALU.mult, ALU.add).then_inc(s_norm, 1)

            def xn_lo_parts(n):
                for k in range(KC):
                    dve.wait_ge(s_xh, n * KC + k + 1)
                    lo_part(xn_lo[:, k, :], x_t[:, k, :], xn_hi[:, k, :], s_xl)

            def t_lo_part(n, c):
                h, j = c // KC, c % KC
                dve.wait_ge(s_hi, n * 2 * NT + c + 1)
                at = (slice(None), j, slice(h * BANK, (h + 1) * BANK))
                nc.vector.scalar_tensor_tensor(out=t_lo[at], in0=work[use_t(0, c) % 2], scalar=wk_bq[:, j:j + 1],
                                               in1=t_hi[at].bitcast(FP32), op0=ALU.add,
                                               op1=ALU.subtract).then_inc(s_free, 1)

            ROW_STEPS = 3

            def row_sums(n):
                nc.vector.tensor_tensor(row_w[:], scale_c[:], wq_bk[:], ALU.mult).then_inc(s_rv, 1)
                nc.vector.tensor_tensor(row_p[:], shift_c[:], wq_bk[:], ALU.mult).then_inc(s_rv, 1)
                dve.wait_ge(s_rv, n * ROW_STEPS + 2)
                nc.vector.reduce_sum(row_s[:], row_p[:], AX.X).then_inc(s_stin, 1)

            def row_spread(n):
                dve.wait_ge(s_stat, n * 4 + 3)
                nc.vector.tensor_tensor(row_0[:], bqbk[:], stat[:, 0:1], ALU.add)
                for k in range(KC):
                    last = nc.vector.tensor_scalar(row_junk[:, k * P:(k + 1) * P], ident[:], row_w[:, k:k + 1],
                                                   None, ALU.mult)
                last.then_inc(s_stin, 1)

            def row_term(n, i):
                if i == 0:
                    dve.wait_ge(s_stat, n * 4 + 4)
                dve.wait_ge(s_rp, n * NT + i)
                nc.vector.tensor_tensor_reduce(out=row_junk[:], in0=x_in[:, i, :], in1=stat, scale=1.0,
                                               scalar=0.0, op0=ALU.mult, op1=ALU.add,
                                               accum_out=row_x[:, i:i + 1]).then_inc(s_rp, 1)

            def row_finish(n):
                dve.wait_ge(s_rp, n * NT + NT)
                nc.vector.tensor_scalar(row[:], row_x[:], row_0[:], None, ALU.add).then_inc(s_rv, 1)
                dve.wait_ge(s_rv, n * ROW_STEPS + 3)
                nc.vector.tensor_scalar(row_scaled[:], row[:], SCALE, None, ALU.mult).then_inc(s_row, 1)

            def pt_lo_part(b, i):
                for g in range(2):
                    dve.wait_ge(s_pth, b * 2 * NT + 2 * i + g + 1)
                    part = slice(g * KC, (g + 1) * KC)
                    lo_part(pt_lo[:, part, :].rearrange("p m n -> p (m n)"), pt_ps[:, g, :],
                            pt_hi[:, part, :].rearrange("p m n -> p (m n)"), s_ptl)

            def tile_top(b, i):
                dve.wait_ge(s_s, b * NT + i + 1)
                nc.vector.reduce_max(top[:, i:i + 1], scores, AX.X).then_inc(s_top, 1)
                dve.wait_ge(s_top, b * NT + i + 1)
                nc.vector.tensor_scalar(top_neg[:, i:i + 1], top[:, i:i + 1], row[:, i:i + 1], -SCALE,
                                        ALU.add, ALU.mult).then_inc(s_topn, 1)
                dve.wait_ge(s_topn, b * NT + i + 1)
                nc.vector.tensor_scalar(exp_bias[:, i:i + 1], top_neg[:, i:i + 1], row_scaled[:, i:i + 1], None,
                                        ALU.add).then_inc(s_eb, 1)

            def tile_out(b, i):
                dve.wait_ge(s_p, b * NT + i + 1)
                nc.vector.reciprocal(total_inv[:, i:i + 1], total[:, i:i + 1]).then_inc(s_ti, 1)
                dve.wait_ge(s_o, b * NT + i + 1)
                dve.wait_ge(s_res, b * NT + i + 1)
                dve.wait_ge(s_ti, b * NT + i + 1)
                nc.vector.scalar_tensor_tensor(out=x_res[:, i, :], in0=o_ps, scalar=total_inv[:, i:i + 1],
                                               in1=x_res[:, i, :], op0=ALU.mult, op1=ALU.add).then_inc(s_y, 1)

            def setup_lo_parts(u0, hi, lo):
                for k in range(KC):
                    dve.wait_ge(s_seth, reads(u0 + k))
                    lo_part(lo[:, k, :], psum[:, (u0 + k) % 4, :], hi[:, k, :], s_setr)

            for i in range(NT):
                x_evict(0, i)
                if i % TH == TH - 1:
                    half_stats(0, i // TH)
            dve.wait_ge(s_sv, NH)
            channel_stats(0)
            group_variance(0)
            dve.wait_ge(s_vec, 1)
            nc.vector.tensor_copy(vec_cols[:], o_ps[:, 0:5 * KC]).then_inc(s_setv, 1)
            dve.wait_ge(s_setv, 1)
            norm(0)
            for k in range(KC):
                nc.vector.tensor_scalar(bv_wide[:, k, :], ones[:], bv_c[:, k:k + 1], None, ALU.mult).then_inc(s_setv, 1)
            nc.vector.tensor_tensor(bq_bk[:], bq_c, bk_c, ALU.mult).then_inc(s_setv, 1)
            dve.wait_ge(s_setv, KC + 2)
            nc.vector.reduce_sum(bqbk_part[:], bq_bk[:], AX.X).then_inc(s_setv, 1)
            setup_lo_parts(SET_A, a_hi, a_lo)
            xn_lo_parts(0)
            setup_lo_parts(SET_M, m_hi, m_lo)
            dve.wait_ge(s_set, SET_VEC + 1)
            vec = psum[:, SET_VEC % 4, :]
            nc.vector.tensor_copy(wk_bq[:], vec[:, 0:KC]).then_inc(s_setv, 1)
            nc.vector.tensor_copy(wq_bk[:], vec[:, KC:2 * KC]).then_inc(s_setv, 1)
            nc.vector.tensor_copy(bqbk[:], vec[:, 2 * KC:2 * KC + 1]).then_inc(s_setr, 1)
            dve.wait_ge(s_set, SET_BIAS + 1)
            nc.vector.tensor_copy(out_bias[:], psum[:, SET_BIAS % 4, :]).then_inc(s_setr, 1)
            t_lo_part(0, 0)

            def image(b, more):
                row_sums(b)
                for c in range(1, NT):
                    t_lo_part(b, c)
                    if c == 1:
                        row_spread(b)
                    if c >= 4:
                        row_term(b, c - 4)
                for m in range(NT):
                    if m == NT - 2:
                        row_finish(b)
                        tile_top(b, 0)
                    dve.wait_ge(s_hi, b * 2 * NT + NT + m + 1)
                    lo_part(v_lo[:, m, :], work[use_v(0, m) % 2], v_hi[:, m, :], s_free)
                    if m < NT // 2:
                        row_term(b, NT // 2 + m)
                for i in range(NT):
                    if more and i == 5:
                        dve.wait_ge(s_sv, (b + 1) * STAT_STEPS + NH)
                    if i >= 2:
                        tile_out(b, i - 2)
                    if more and i == 5:
                        channel_stats(b + 1)
                    if i >= 1:
                        pt_lo_part(b, i - 1)
                    if i == 1 and more:
                        x_evict(b + 1, 0)
                        x_evict(b + 1, 1)
                    if i >= 1:
                        tile_top(b, i)
                    if more:
                        if 1 <= i < NT // 2:
                            x_evict(b + 1, 2 * i)
                            x_evict(b + 1, 2 * i + 1)
                        if i == 1:
                            half_stats(b + 1, 0)
                        if i == 4:
                            half_stats(b + 1, 1)
                        if i == 5:
                            group_variance(b + 1)
                        if i == 6:
                            norm(b + 1)
                if more:
                    xn_lo_parts(b + 1)
                tile_out(b, NT - 2)
                pt_lo_part(b, NT - 1)
                if more:
                    t_lo_part(b + 1, 0)
                tile_out(b, NT - 1)

            if B > 1:
                with dve.Fori(0, B - 1) as b:
                    image(b, True)
            image(B - 1, False)

        @block.tensor
        def _(pe):
            def product(dst, pairs, xn_ready=None):
                for n, (s_hi_, s_lo_, m_hi_, m_lo_) in enumerate(pairs):
                    if xn_ready is not None:
                        pe.wait_ge(s_xl, xn_ready * KC + n + 1)
                    nc.tensor.matmul(dst, s_hi_, m_hi_, start=n == 0, stop=False)
                    nc.tensor.matmul(dst, s_hi_, m_lo_, start=False, stop=False)
                    last = nc.tensor.matmul(dst, s_lo_, m_hi_, start=False, stop=n == len(pairs) - 1)
                return last

            def chunk(c):
                return slice(c * P, (c + 1) * P)

            def setup_bank(u):
                if u >= 4:
                    pe.wait_ge(s_wt if weight_use(u - 4) else s_setr, reads(u - 4))
                return psum[:, u % 4, :]

            def weight_transpose(u0, w, loaded):
                pe.wait_ge(loaded, 16)
                for j in range(KC):
                    bank = setup_bank(u0 + j)
                    for k in range(KC):
                        last = nc.tensor.transpose(bank[:, chunk(k)], w[:, k, chunk(j)], ident[:])
                    last.then_inc(s_set, 1)

            def weight_product(u0, left, right):
                for k in range(KC):
                    bank = setup_bank(u0 + k)
                    if k == 0:
                        pe.wait_ge(s_wt, reads(u0 - 1))
                    for j in range(KC):
                        last = nc.tensor.matmul(bank, left[:, j, chunk(k)], right[:, j, :],
                                                start=j == 0, stop=j == KC - 1)
                    last.then_inc(s_set, 1)

            def work_bank(use, parity):
                pe.wait_ge(s_free, use - 1)
                return work[parity % 2]

            def x_transpose(n, i):
                use = use_x(n, i)
                if i % TH == 0:
                    pe.wait_ge(s_x[i // TH], n * 16 + 16)
                bank = work[i % 2] if isinstance(n, int) and n == 0 and i < 2 else work_bank(use, i)
                for k in range(KC):
                    last = nc.tensor.transpose(bank[:, chunk(k)], x_in[:, i, chunk(k)], ident[:])
                last.then_inc(s_work, 1)

            def group_sum(n, step, rhs):
                pe.wait_ge(s_stin, n * 4 + step + 1)
                nc.tensor.matmul(stat[:, 0:KC], group_avg[:], rhs, start=True, stop=True).then_inc(s_stat, 1)

            def t_chunk(n, c):
                h, j = c // KC, c % KC
                tokens = slice(h * BANK, (h + 1) * BANK)
                dst = work_bank(use_t(n, c), use_t(0, c))
                product(dst, [(a_hi[:, k, chunk(j)], a_lo[:, k, chunk(j)], xn_hi[:, k, tokens], xn_lo[:, k, tokens])
                              for k in range(KC)], xn_ready=n if c == 0 else None).then_inc(s_work, 1)

            def v_tile(n, m):
                dst = work_bank(use_v(n, m), use_v(0, m))
                product(dst, [(xn_hi[:, k, chunk(m)], xn_lo[:, k, chunk(m)], m_hi[:, k, :], m_lo[:, k, :])
                              for k in range(KC)]).then_inc(s_work, 1)

            def score_tile(b, i):
                if i == 0:
                    pe.wait_ge(s_free, use_v(b, 0))
                for h in range(NH):
                    tokens = slice(h * BANK, (h + 1) * BANK)
                    last = product(scores[:, tokens], [(t_hi[:, k, chunk(i)], t_lo[:, k, chunk(i)],
                                                        xn_hi[:, k, tokens], xn_lo[:, k, tokens]) for k in range(KC)])
                last.then_inc(s_s, 1)

            def prob_transpose(b, i):
                pe.wait_ge(s_p, b * NT + i + 1)
                for m in range(NT):
                    last = nc.tensor.transpose(pt_ps[:, m // KC, chunk(m % KC)], prob[:, chunk(m)], ident[:])
                    if m % KC == KC - 1:
                        last.then_inc(s_pt, 1)

            def out_tile(b, i):
                if i == 0:
                    pe.wait_ge(s_free, use_v(b, NT - 1) + 1)
                pe.wait_ge(s_y, b * NT + i)
                for m in range(NT):
                    if m % KC == 0:
                        pe.wait_ge(s_ptl, b * 2 * NT + 2 * i + m // KC + 1)
                    nc.tensor.matmul(o_ps, pt_hi[:, m, :], v_hi[:, m, :], start=m == 0, stop=False)
                    nc.tensor.matmul(o_ps, pt_hi[:, m, :], v_lo[:, m, :], start=False, stop=False)
                    last = nc.tensor.matmul(o_ps, pt_lo[:, m, :], v_hi[:, m, :], start=False, stop=m == NT - 1)
                last.then_inc(s_o, 1)

            pe.wait_ge(s_const, 6)
            for i in range(NT):
                x_transpose(0, i)
            weight_transpose(SET_WQ, w_q, s_wload[0])
            weight_transpose(SET_WK, w_k, s_wload[1])
            pe.wait_ge(s_small, 16 * 6)
            nc.tensor.transpose(o_ps[:, 0:5 * KC], vec_rows[:], ident[0:5 * KC, 0:5 * KC]).then_inc(s_vec, 1)
            group_sum(0, 0, mv[:, :, 0])
            weight_product(SET_A, wq_t, wk_t)
            group_sum(0, 1, dev[:])
            weight_transpose(SET_WV, w_v, s_wload[2])
            pe.wait_ge(s_wload[3], 16)
            weight_product(SET_M, wv_t, w_p)
            bank = setup_bank(SET_VEC)
            pe.wait_ge(s_setv, KC + 3)
            for n, (w_t, vec) in enumerate(((wk_t, bq_c), (wq_t, bk_c))):
                for k in range(KC):
                    for j in range(KC):
                        nc.tensor.matmul(bank[:, n * KC + k:n * KC + k + 1], w_t[:, j, chunk(k)], vec[:, j:j + 1],
                                         start=j == 0, stop=j == KC - 1)
            nc.tensor.matmul(bank[:, 2 * KC:2 * KC + 1], ones[:], bqbk_part[:], start=True, stop=True).then_inc(s_set, 1)
            bank = setup_bank(SET_BIAS)
            for j in range(KC):
                nc.tensor.matmul(bank, bv_wide[:, j, :], w_p[:, j, :], start=j == 0, stop=False)
            nc.tensor.matmul(bank, ones[0:1, :], bp_row[:], start=False, stop=True).then_inc(s_set, 1)
            pe.wait_ge(s_setr, reads(SET_M + KC - 1))
            t_chunk(0, 0)

            def image(b, more):
                for c in range(1, NT):
                    t_chunk(b, c)
                    if c == 1:
                        pe.wait_ge(s_stin, b * 4 + 3)
                        nc.tensor.matmul(stat[:, 0:1], ones[:], row_s[:], start=True, stop=True).then_inc(s_stat, 1)
                    if c == 3:
                        pe.wait_ge(s_stin, b * 4 + 4)
                        nc.tensor.matmul(stat, ones[:], row_junk[:], start=True, stop=True).then_inc(s_stat, 1)
                for m in range(NT):
                    if m == NT - 2:
                        score_tile(b, 0)
                    v_tile(b, m)
                for i in range(NT):
                    if i >= 1:
                        prob_transpose(b, i - 1)
                        if i == 1 and more:
                            x_transpose(b + 1, 0)
                            x_transpose(b + 1, 1)
                        score_tile(b, i)
                    if more:
                        if 1 <= i < NT // 2:
                            x_transpose(b + 1, 2 * i)
                            x_transpose(b + 1, 2 * i + 1)
                        if i == 5:
                            group_sum(b + 1, 0, mv[:, :, 0])
                        if i == 6:
                            group_sum(b + 1, 1, dev[:])
                    if i >= 1:
                        out_tile(b, i - 1)
                prob_transpose(b, NT - 1)
                if more:
                    t_chunk(b + 1, 0)
                out_tile(b, NT - 1)

            if B > 1:
                with pe.Fori(0, B - 1) as b:
                    image(b, True)
            image(B - 1, False)


_INS = ["x"] + ["L0_conv_" + n for n in ("gamma", "beta", "wq", "bq", "wk", "bk", "wv", "bv", "wp", "bp")]


def kernel(**inputs):
    import numpy as _np
    import concourse.bacc as _bacc
    from concourse.bass_utils import run_bass_kernel_spmd as _run

    nc = _bacc.Bacc("TRN2", target_bir_lowering=False, num_devices=1)
    arrays, args = {}, []
    for name in _INS:
        a = _np.ascontiguousarray(inputs[name])
        arrays[f"in_{name}_dram"] = a
        args.append(nc.dram_tensor(f"in_{name}_dram", a.shape, mybir.dt.from_np(a.dtype), kind="ExternalInput").ap())
    args.append(nc.dram_tensor("out_dram", inputs["x"].shape, FP32, kind="ExternalOutput").ap())
    group_norm_attention(nc, *args)
    r = _run(nc, [arrays], core_ids=[0])
    return r.results[0]["out_dram"]
```

```python
import concourse.bass as bass
from concourse import mybir
from contextlib import ExitStack

FP32 = mybir.dt.float32
F32R = mybir.dt.float32r
ALU = mybir.AluOpType
ACT = mybir.ActivationFunctionType

MAX = bass.bass_isa.ReduceOp.max
ADD = bass.bass_isa.ReduceOp.add

P = 128
BANK = 512
GROUPS = 32
EPS = 0.001


def group_norm_attention(nc, x, gamma, beta, wq, bq, wk, bk, wv, bv, wp, bp, out):
    B, H, W, C = x.shape
    N = H * W
    KC = C // P
    NT = N // P
    NH = N // BANK
    TH = NT // NH
    PG = P // (C // GROUPS)
    CG = C // GROUPS
    SCALE = float(C) ** -0.5
    assert C == BANK and N == 2 * BANK and NT % 2 == 0

    x_rows = x.rearrange("b h w c -> b (h w) c").rearrange("b (t p) c -> b p t c", p=P)
    SQ = 32
    NI = P // SQ
    NQ = 4
    TQ = N // NQ
    assert NI == KC and SQ % CG == 0
    x_quarters = x.rearrange("b h w c -> b (h w) c").rearrange("b (q j t) (i r) -> b q i t j r", q=NQ, t=SQ, i=NI)
    out_rows = out.rearrange("b h w c -> b (h w) c").rearrange("b (t p) c -> b p t c", p=P)

    ctx = ExitStack()
    with ctx:
        def sb(name, shape, dt=FP32, where=ctx):
            return where.enter_context(nc.sbuf_tensor(name, shape, dt))

        def sem(name):
            return ctx.enter_context(nc.semaphore(name))

        ident = sb("ident", [P, P])
        ones = sb("ones", [P, P])
        group_avg = sb("group_avg", [P, P])
        vec_cols = sb("vec_cols", [P, 3 * KC])
        gamma_c, beta_c, bv_c = (vec_cols[:, n * KC:(n + 1) * KC] for n in range(3))
        minus_half = sb("minus_half", [P, KC])
        wk_bq = sb("wk_bq", [P, KC])
        wq_bk = sb("wq_bk", [P, KC])
        bqbk = sb("bqbk", [P, 1])
        bqbk_part = sb("bqbk_part", [P, 1])
        out_bias = sb("out_bias", [P, C])

        x_res = sb("x_res", [P, TH, C])
        x_blk = sb("x_blk", [P, 2, TQ // SQ * P])
        x_t = sb("x_t", [P, KC, N])
        xn_hi = sb("xn_hi", [P, KC, N], F32R)
        xn_lo = sb("xn_lo", [P, KC, N], F32R)
        a_hi = sb("a_hi", [P, KC, C], F32R)
        a_lo = sb("a_lo", [P, KC, C], F32R)
        m_hi = sb("m_hi", [P, KC, C], F32R)
        m_lo = sb("m_lo", [P, KC, C], F32R)
        score = sb("score", [P, NT, BANK])
        top_part = sb("top_part", [P, BANK])
        shift = sb("shift", [P, BANK])
        total_part = sb("total_part", [P, BANK])
        row = sb("row", [P, N])
        bn = sb("bn", [P, KC, NH, 6])
        mv = sb("mv", [P, KC, 2])
        g_mean = sb("g_mean", [P, KC])
        dev = sb("dev", [P, KC])
        g_var = sb("g_var", [P, KC])
        rstd = sb("rstd", [P, KC])
        scale_c = sb("scale_c", [P, KC])
        shift_c = sb("shift_c", [P, KC])
        total = sb("total", [P, NT])
        total_inv = sb("total_inv", [P, NT])

        with ExitStack() as setup:
            vec_rows = sb("vec_rows", [3 * KC, P], where=setup)
            w_v = sb("w_v", [P, KC, C], where=setup)
            wv_t_lo, wv_t_hi, wp_lo, wp_hi = (sb(n, [P, KC, C], F32R, where=setup)
                                              for n in ("wv_t_lo", "wv_t_hi", "wp_lo", "wp_hi"))
            w_p, w_k, w_q = (sb(n, [P, KC, C], where=setup) for n in ("w_p", "w_k", "w_q"))
            bq_wide, bk_wide, bp_wide = (sb(n, [P, C], where=setup) for n in ("bq_wide", "bk_wide", "bp_wide"))
            products = sb("products", [P, C], where=setup)
            bias_part = sb("bias_part", [P, C], where=setup)
        (wq_t_hi, wq_t_lo), (wk_t_hi, wk_t_lo) = ([part[:, :, half * C:(half + 1) * C] for part in (xn_hi, xn_lo)]
                                                  for half in range(2))
        t_hi = sb("t_hi", [P, KC, BANK], F32R)
        t_lo = sb("t_lo", [P, KC, BANK], F32R)
        v_hi = sb("v_hi", [P, NT, C], F32R)
        v_lo = sb("v_lo", [P, NT, C], F32R)
        pt_hi = sb("pt_hi", [P, NT, BANK], F32R)
        pt_lo = sb("pt_lo", [P, NT, BANK], F32R)

        psum = ctx.enter_context(nc.psum_tensor("psum", [P, 8, BANK], FP32))
        work = [psum[:, n, :] for n in range(4)]
        o_ps = [psum[:, 4, :], psum[:, 5, :]]
        stat = psum[:, 7, :]
        vec_ps = stat[:, KC:4 * KC]

        s_wload = [sem(f"w_loaded{i}") for i in range(4)]
        s_small = sem("small_loaded")
        s_wide = sem("wide_vectors_loaded")
        s_vec = sem("vectors_transposed")
        s_const = sem("constants_made")
        s_set = sem("setup_product_done")
        s_seth = sem("setup_hi_ready")
        s_setr = sem("setup_lo_ready")
        s_wph = sem("wp_hi_ready")
        s_wpl = sem("wp_lo_ready")
        s_bias = sem("out_bias_step")
        s_setv = sem("setup_vector_step")
        s_xb = [sem(f"x_quarter{q}_loaded") for q in range(NQ)]
        s_tr = sem("x_quarter_transposed")
        s_xr = [sem(f"x_tile_loaded_in_{i}") for i in range(TH)]
        s_res = sem("residual_ready")
        s_work = sem("work_bank_full")
        s_hi = sem("t_or_v_hi_ready")
        s_free = sem("t_or_v_lo_ready")
        s_sr = sem("scores_in_sbuf")
        s_stin = sem("stat_input_ready")
        s_stat = sem("stat_bank_full")
        s_sv = sem("stat_step")
        s_pw_in = sem("variance_ready")
        s_pw = sem("rstd_ready")
        s_norm = sem("chunk_normed")
        s_xh = sem("xn_hi_ready")
        s_xl = sem("xn_lo_ready")
        s_rv = sem("row_sum_step")
        s_r = sem("row_ready")
        s_mx = sem("top_part_step")
        s_par = sem("top_ready")
        s_sh = sem("shift_ready")
        s_sub = sem("score_shifted")
        s_p = sem("prob_ready")
        s_pth = sem("pt_hi_ready")
        s_ptl = sem("pt_lo_ready")
        s_sum = sem("total_part_step")
        s_tt = sem("total_ready")
        s_tot = sem("total_in_its_partition")
        s_ti = sem("total_inv_ready")
        s_o = sem("o_done")
        s_y = sem("out_tile_ready")
        s_st = [sem(f"out_tile_stored_from_{i}") for i in range(TH)]

        block = ctx.enter_context(nc.Block())

        USES = ([("t", 0, j) for j in range(KC)] + [("v", 0, m) for m in range(2)]
                + [("s", 0, m) for m in range(NT)] + [("t", 1, j) for j in range(KC)]
                + [("v", 0, m) for m in range(2, NT)] + [("s", 1, m) for m in range(NT)])
        NU = len(USES)
        SPLIT, SCORES = 2 * NT, NH * NT
        PLACE = {u: sum((w[0] == "s") == (u[0] == "s") for w in USES[:n]) for n, u in enumerate(USES)}
        assert NU % 4 == 0 and NU == SPLIT + SCORES

        def starts(n, h=0):
            return h == 0 and isinstance(n, int) and n == 0

        def use(n, *what):
            return n * NU + USES.index(what) + 1

        def bank_of(*what):
            return work[USES.index(what) % 4]

        def quarter_of(n, q):
            if starts(n):
                return score[:, q * NT // NQ:(q + 1) * NT // NQ, :].rearrange("p m n -> p (m n)")
            return x_blk[:, q % 2, :]

        SET_BANKS = 7
        SET_WQ, SET_WK, SET_A, SET_WV, SET_M = (n * KC for n in range(5))

        SETV_WK_BQ = KC + 1
        SETV_VECTORS = 2 * KC + 3
        BIAS_STEPS = 2 * KC + 1
        STAT_STEPS = 6
        SHIFTED = {("t", 3): (0, 2), ("v", 2): (2, 4), ("v", 3): (4, 6), ("v", 4): (6, NT)}
        SPLIT_UP = {("v", 5): (0, 2), ("v", 6): (2, 5), ("v", 7): (5, NT)}

        TRANSPOSED = {("v", 1): 0, ("s", 2): 1, ("s", 6): 2, ("t", 0): 3}
        MEASURED = {("s", 3): (0, 0, 2), ("s", 4): (0, 2, KC), ("t", 1): (1, 0, 2), ("t", 2): (1, 2, KC)}

        @block.sync
        def _(sp):
            def load_quarter(n, q):
                for i in range(NI):
                    sp.dma_start(quarter_of(n, q)[i * SQ:(i + 1) * SQ, :].rearrange("t (j r) -> t j r", r=P),
                                 x_quarters[n, q, i]).then_inc(s_xb[q], 16)

            def load_tile(n, i):
                if not starts(n, i // TH):
                    sp.wait_ge(s_st[i % TH], 16 * (NH * n + i // TH))
                sp.dma_start(x_res[:, i % TH, :], x_rows[n, :, i, :]).then_inc(s_xr[i % TH], 16)

            def store_tile(n, i):
                sp.wait_ge(s_y, n * NT + i + 1)
                sp.dma_start(out_rows[n, :, i, :], x_res[:, i % TH, :]).then_inc(s_st[i % TH], 16)

            def load_weight(w, dst, loaded):
                for i in range(NI):
                    sp.dma_start(dst[i * SQ:(i + 1) * SQ, :, :],
                                 w.rearrange("(i k a) n -> i a k n", i=NI, k=KC)[i]).then_inc(loaded, 16)

            load_weight(wq, w_q, s_wload[0])
            load_weight(wk, w_k, s_wload[1])
            for q in range(NQ):
                load_quarter(0, q)
            load_weight(wv, w_v, s_wload[2])
            sp.dma_start(w_p[:], wp.rearrange("(k p) n -> p k n", p=P)).then_inc(s_wload[3], 16)
            for vec, dst in ((bq, bq_wide), (bk, bk_wide), (bp, bp_wide)):
                sp.dma_start(dst[:], vec.partition_broadcast(P)).then_inc(s_wide, 16)
            if B > 1:
                for q in range(2):
                    sp.wait_ge(s_tr, q + 1)
                    load_quarter(1, q)

            def image(b, images_left):
                for i in range(TH):
                    load_tile(b, i)
                if images_left > 0:
                    for q in range(2, NQ):
                        sp.wait_ge(s_tr, (b + 1) * NQ + q - 1)
                        load_quarter(b + 1, q)
                for i in range(TH):
                    store_tile(b, i)
                    load_tile(b, i + TH)
                if images_left > 1:
                    for q in range(2):
                        sp.wait_ge(s_tr, (b + 2) * NQ + q - 1)
                        load_quarter(b + 2, q)
                for i in range(TH, NT):
                    store_tile(b, i)

            if B > 2:
                image(0, 2)
            if B > 3:
                with sp.Fori(1, B - 2) as b:
                    image(b, 2)
            for b in range(max(B - 2, 0), B):
                image(b, B - 1 - b)
            for i in range(TH):
                sp.wait_ge(s_st[i], 16 * NH * B)

        @block.gpsimd
        def _(pool):
            nc.gpsimd.memset(ones[:], 1.0).then_inc(s_const, 1)
            nc.gpsimd.memset(group_avg[:], 1.0 / CG).then_inc(s_const, 1)
            nc.gpsimd.memset(minus_half[:], -0.5).then_inc(s_const, 1)
            pool.wait_ge(s_const, 3)
            nc.gpsimd.affine_select(out=ident[:], in_=ones[:], compare_op=ALU.is_equal, fill=0.0, base=0,
                                    pattern=[[-1, P]], channel_multiplier=1).then_inc(s_const, 1)
            g = group_avg[:].rearrange("p (g c) -> p g c", c=CG)
            nc.gpsimd.affine_select(out=g, in_=g, compare_op=ALU.is_ge, fill=0.0, base=0,
                                    pattern=[[-CG, PG], [0, CG]], channel_multiplier=1).then_inc(s_const, 1)
            pool.wait_ge(s_const, 5)
            nc.gpsimd.affine_select(out=g, in_=g, compare_op=ALU.is_ge, fill=0.0, base=CG - 1,
                                    pattern=[[CG, PG], [0, CG]], channel_multiplier=-1).then_inc(s_const, 1)

            def root(n):
                pool.wait_ge(s_pw_in, n + 1)
                nc.gpsimd.tensor_tensor(rstd[:], g_var[:], minus_half[:], ALU.pow).then_inc(s_pw, 1)

            def residual(n, i, first=0, end=C):
                pool.wait_ge(s_xr[i % TH], 16 * (NH * n + i // TH + 1))
                at = x_res[:, i % TH, first:end]
                last = nc.gpsimd.tensor_tensor(at, at, out_bias[:, first:end], ALU.add)
                if end == C:
                    last.then_inc(s_res, 1)

            def await_top_part(n, h):
                pool.wait_ge(s_mx, (n * NH + h + 1) * (NT - 1))
                if not starts(n, h):
                    pool.wait_ge(s_sub, (n * NH + h) * NT)

            def top(n, h):
                nc.gpsimd.partition_all_reduce(shift[:], top_part[:], P, MAX).then_inc(s_par, 1)

            def totals(n, h):
                if not starts(n, h):
                    pool.wait_ge(s_ti, n * NH + h)
                for m in range(1, NT):
                    pool.wait_ge(s_p, (n * NH + h) * NT + m + 1)
                    if m > 1:
                        pool.wait_ge(s_sum, (n * NH + h) * (NT - 1) + m - 1)
                    nc.gpsimd.tensor_tensor(total_part[:], score[:, 0, :] if m == 1 else total_part[:],
                                            score[:, m, :], ALU.add).then_inc(s_sum, 1)

            def await_total_part(n, h):
                pool.wait_ge(s_sum, (n * NH + h + 1) * (NT - 1))

            def total_sum():
                nc.gpsimd.partition_all_reduce(total_part[:], total_part[:], P, ADD).then_inc(s_tt, 1)

            def row_sum(n):
                nc.gpsimd.partition_all_reduce(row[:], row[:], P, ADD).then_inc(s_r, 1)

            for k in range(KC):
                pool.wait_ge(s_wph, k + 1)
                nc.gpsimd.tensor_tensor(wp_lo[:, k, :], w_p[:, k, :], wp_hi[:, k, :].bitcast(FP32),
                                        ALU.subtract).then_inc(s_wpl, 1)
            root(0)
            pool.wait_ge(s_wload[3], 16)
            for k in range(KC):
                if k > 1:
                    pool.wait_ge(s_bias, 2 * k - 1)
                nc.gpsimd.tensor_scalar(bias_part[:] if k else out_bias[:], w_p[:, k, :], bv_c[:, k:k + 1], None,
                                        ALU.mult).then_inc(s_bias, 1)
                if k:
                    pool.wait_ge(s_bias, 2 * k)
                    nc.gpsimd.tensor_tensor(out_bias[:], out_bias[:], bias_part[:], ALU.add).then_inc(s_bias, 1)
            pool.wait_ge(s_bias, 2 * KC - 1)
            nc.gpsimd.partition_all_reduce(out_bias[:], out_bias[:], P, ADD).then_inc(s_bias, 1)
            pool.wait_ge(s_wide, 16 * 3)
            pool.wait_ge(s_bias, 2 * KC)
            nc.gpsimd.tensor_tensor(out_bias[:], out_bias[:], bp_wide[:], ALU.add).then_inc(s_bias, 1)
            pool.wait_ge(s_rv, KC)
            row_sum(0)
            pool.wait_ge(s_bias, BIAS_STEPS)

            def image(b, more):
                residual(b, 0)
                residual(b, 1)
                await_top_part(b, 0)
                residual(b, 2)
                top(b, 0)
                totals(b, 0)
                await_total_part(b, 0)
                residual(b, 3, 0, C // 2)
                total_sum()
                if more:
                    root(b + 1)
                await_top_part(b, 1)
                residual(b, 3, C // 2)
                top(b, 1)
                totals(b, 1)
                await_total_part(b, 1)
                residual(b, TH)
                total_sum()
                for i in range(TH + 1, NT):
                    if more and i == NT - 1:
                        pool.wait_ge(s_rv, (b + 2) * KC)
                    residual(b, i)
                if more:
                    row_sum(b + 1)

            if B > 1:
                image(0, True)
            if B > 2:
                with pool.Fori(1, B - 1) as b:
                    image(b, True)
            image(B - 1, False)

        @block.scalar
        def _(act):
            for n, vec in enumerate((gamma, beta)):
                act.dma_start(vec_rows[n * KC:(n + 1) * KC, :].rearrange("k (i a) -> k i a", a=SQ),
                              vec.rearrange("(i k a) -> k i a", i=NI, k=KC)).then_inc(s_small, 16)
            act.dma_start(vec_rows[2 * KC:3 * KC, :], bv.rearrange("(k p) -> k p", p=P)).then_inc(s_small, 16)

            def xn_split(n):
                for k in range(KC):
                    act.wait_ge(s_norm, n * KC + k + 1)
                    nc.scalar.activation(xn_hi[:, k, :], x_t[:, k, :], ACT.Copy).then_inc(s_xh, 1)

            def hi_part(n, *what):
                kind, h, j = what
                act.wait_ge(s_work, use(n, *what))
                if kind == "t":
                    nc.scalar.activation(t_hi[:, j, :], bank_of(*what), ACT.Identity,
                                         bias=wk_bq[:, j:j + 1]).then_inc(s_hi, 1)
                else:
                    nc.scalar.activation(v_hi[:, j, :], bank_of(*what), ACT.Copy).then_inc(s_hi, 1)

            def scores_out(n, h):
                for m in range(NT):
                    if h:
                        act.wait_ge(s_ptl, (n * NH + h - 1) * NT + m + 1)
                        act.wait_ge(s_sum, (n * NH + h - 1) * (NT - 1) + max(m, 1))
                    elif m == 0 and not starts(n):
                        act.wait_ge(s_ptl, n * NH * NT)
                        act.wait_ge(s_sum, n * NH * (NT - 1))
                    act.wait_ge(s_work, use(n, "s", h, m))
                    nc.scalar.activation(score[:, m, :], bank_of("s", h, m), ACT.Copy).then_inc(s_sr, 1)

            def exps(n, h, first, end):
                for m in range(first, end):
                    act.wait_ge(s_sub, (n * NH + h) * NT + m + 1)
                    nc.scalar.activation(score[:, m, :], score[:, m, :], ACT.Exp, scale=SCALE).then_inc(s_p, 1)

            def pt_hi_parts(n, h, first, end):
                if first == 0 and end and not starts(n, h):
                    act.wait_ge(s_o, n * NT + h * TH)
                for m in range(first, end):
                    act.wait_ge(s_p, (n * NH + h) * NT + m + 1)
                    nc.scalar.activation(pt_hi[:, m, :], score[:, m, :], ACT.Copy).then_inc(s_pth, 1)

            def setup_hi_parts(u0, dst, first=0, end=KC):
                for k in range(first, end):
                    act.wait_ge(s_set, u0 + k + 1)
                    nc.scalar.activation(dst[:, k, :], psum[:, (u0 + k) % SET_BANKS, :], ACT.Copy).then_inc(s_seth, 1)

            setup_hi_parts(SET_WQ, wq_t_hi)
            setup_hi_parts(SET_WK, wk_t_hi)
            setup_hi_parts(SET_A, a_hi)
            act.wait_ge(s_wload[3], 16)
            for k in range(KC):
                nc.scalar.activation(wp_hi[:, k, :], w_p[:, k, :], ACT.Copy).then_inc(s_wph, 1)
                if k == 1:
                    setup_hi_parts(SET_WV, wv_t_hi)
            setup_hi_parts(SET_M, m_hi, 0, 1)
            xn_split(0)
            setup_hi_parts(SET_M, m_hi, 1, KC)
            act.wait_ge(s_setv, SETV_WK_BQ)
            for j in range(KC):
                hi_part(0, "t", 0, j)
            act.wait_ge(s_setv, SETV_VECTORS)
            act.wait_ge(s_bias, BIAS_STEPS)

            def image(b, more):
                hi_part(b, "v", 0, 0)
                hi_part(b, "v", 0, 1)
                scores_out(b, 0)
                for j in range(KC):
                    hi_part(b, "t", 1, j)
                    exps(b, 0, *SHIFTED.get(("t", j), (0, 0)))
                for m in range(2, NT):
                    hi_part(b, "v", 0, m)
                    exps(b, 0, *SHIFTED.get(("v", m), (0, 0)))
                    pt_hi_parts(b, 0, *SPLIT_UP.get(("v", m), (0, 0)))
                scores_out(b, 1)
                if more:
                    act.wait_ge(s_work, use(b, "s", 1, NT - 1))
                    xn_split(b + 1)
                exps(b, 1, 0, NT)
                for j in range(KC):
                    pt_hi_parts(b, 1, 2 * j, 2 * j + 2)
                    if more:
                        hi_part(b + 1, "t", 0, j)

            if B > 1:
                image(0, True)
            if B > 2:
                with act.Fori(1, B - 1) as b:
                    image(b, True)
            image(B - 1, False)

        @block.vector
        def _(dve):
            def lo_part(dst, src, hi, signal):
                nc.vector.tensor_tensor(dst, src, hi.bitcast(FP32), ALU.subtract).then_inc(signal, 1)

            def quarter_transpose(n, q):
                if q == 0 and not starts(n):
                    dve.wait_ge(s_rv, n * KC)
                dve.wait_ge(s_xb[q], (n + 1) * 16 * NI)
                blocks = quarter_of(n, q).rearrange("p (j k a) -> p k j a", k=KC, a=SQ)
                for k in range(KC):
                    last = nc.vector.transpose(
                        x_t[:, k, q * TQ:(q + 1) * TQ].rearrange("p (j t) -> p j t", t=SQ), blocks[:, k])
                last.then_inc(s_tr, 1)

            def token_stats(n, h, first, end):
                dve.wait_ge(s_tr, n * NQ + (h + 1) * NQ // NH)
                for k in range(first, end):
                    last = nc.vector.bn_stats(bn[:, k, h, :], x_t[:, k, h * BANK:(h + 1) * BANK])
                if h == NH - 1 and end == KC:
                    last.then_inc(s_sv, 1)

            def channel_stats(n):
                for k in range(KC):
                    last = nc.vector.bn_aggr(mv[:, k, :], bn[:, k, :, :].rearrange("p h s -> p (h s)"))
                last.then_inc(s_stin, 1)

            def group_variance(n):
                dve.wait_ge(s_stin, n * 2 + 1)
                dve.wait_ge(s_stat, n * 2 + 1)
                nc.vector.tensor_copy(g_mean[:], stat[:, 0:KC])
                nc.vector.tensor_tensor(dev[:], mv[:, :, 0], stat[:, 0:KC], ALU.subtract).then_inc(s_sv, 1)
                dve.wait_ge(s_sv, n * STAT_STEPS + 2)
                nc.vector.tensor_tensor(dev[:], dev[:], dev[:], ALU.mult).then_inc(s_sv, 1)
                dve.wait_ge(s_sv, n * STAT_STEPS + 3)
                nc.vector.tensor_tensor(dev[:], dev[:], mv[:, :, 1], ALU.add).then_inc(s_stin, 1)

            def variance(n):
                dve.wait_ge(s_stat, n * 2 + 2)
                nc.vector.tensor_scalar(g_var[:], stat[:, 0:KC], EPS, None, ALU.add).then_inc(s_pw_in, 1)

            def norm(n):
                dve.wait_ge(s_pw, n + 1)
                nc.vector.tensor_tensor(scale_c[:], rstd[:], gamma_c, ALU.mult).then_inc(s_sv, 1)
                dve.wait_ge(s_sv, n * STAT_STEPS + 4)
                nc.vector.tensor_tensor(dev[:], g_mean[:], scale_c[:], ALU.mult).then_inc(s_sv, 1)
                dve.wait_ge(s_sv, n * STAT_STEPS + 5)
                nc.vector.tensor_tensor(shift_c[:], beta_c, dev[:], ALU.subtract).then_inc(s_sv, 1)
                dve.wait_ge(s_sv, n * STAT_STEPS + 6)
                for k in range(KC):
                    nc.vector.tensor_scalar(x_t[:, k, :], x_t[:, k, :], scale_c[:, k:k + 1], shift_c[:, k:k + 1],
                                            ALU.mult, ALU.add).then_inc(s_norm, 1)

            def row_part(n, k):
                dve.wait_ge(s_norm, n * KC + k + 1)
                if k == 0:
                    nc.vector.tensor_scalar(row[:], x_t[:, 0, :], wq_bk[:, 0:1], bqbk_part[:],
                                            ALU.mult, ALU.add).then_inc(s_rv, 1)
                else:
                    dve.wait_ge(s_rv, n * KC + k)
                    nc.vector.scalar_tensor_tensor(out=row[:], in0=x_t[:, k, :], scalar=wq_bk[:, k:k + 1],
                                                   in1=row[:], op0=ALU.mult, op1=ALU.add).then_inc(s_rv, 1)

            def xn_lo_parts(n):
                for k in range(KC):
                    dve.wait_ge(s_xh, n * KC + k + 1)
                    lo_part(xn_lo[:, k, :], x_t[:, k, :], xn_hi[:, k, :], s_xl)

            def split_lo_part(n, *what):
                kind, h, j = what
                dve.wait_ge(s_hi, n * SPLIT + PLACE[what] + 1)
                if kind == "t":
                    nc.vector.scalar_tensor_tensor(out=t_lo[:, j, :], in0=bank_of(*what), scalar=wk_bq[:, j:j + 1],
                                                   in1=t_hi[:, j, :].bitcast(FP32), op0=ALU.add,
                                                   op1=ALU.subtract).then_inc(s_free, 1)
                else:
                    lo_part(v_lo[:, j, :], bank_of(*what), v_hi[:, j, :], s_free)

            def top_part_step(n, h, m):
                dve.wait_ge(s_sr, (n * NH + h) * NT + m + 1)
                if m == 1:
                    if not starts(n, h):
                        dve.wait_ge(s_par, n * NH + h)
                elif m > 1:
                    dve.wait_ge(s_mx, (n * NH + h) * (NT - 1) + m - 1)
                if m:
                    nc.vector.tensor_tensor(top_part[:], score[:, 0, :] if m == 1 else top_part[:],
                                            score[:, m, :], ALU.max).then_inc(s_mx, 1)

            def tile_shift(n, h):
                dve.wait_ge(s_r, n + 1)
                dve.wait_ge(s_par, n * NH + h + 1)
                own = row[:, h * BANK:(h + 1) * BANK]
                nc.vector.tensor_tensor(shift[:], shift[:], own, ALU.add).then_inc(s_sh, 1)
                dve.wait_ge(s_sh, 2 * (n * NH + h) + 1)
                nc.vector.tensor_tensor(shift[:], own, shift[:], ALU.subtract).then_inc(s_sh, 1)

            def shifts(n, h, first, end):
                for m in range(first, end):
                    if m == first:
                        dve.wait_ge(s_sh, 2 * (n * NH + h) + 2)
                    nc.vector.tensor_tensor(score[:, m, :], score[:, m, :], shift[:], ALU.add).then_inc(s_sub, 1)

            def pt_lo_parts(n, h, first, end):
                for m in range(first, end):
                    dve.wait_ge(s_pth, (n * NH + h) * NT + m + 1)
                    lo_part(pt_lo[:, m, :], score[:, m, :], pt_hi[:, m, :], s_ptl)

            def totals(n, h):
                tiles = slice(h * TH, (h + 1) * TH)
                dve.wait_ge(s_tt, n * NH + h + 1)
                for i in range(TH):
                    sums = total_part[:, i * P:(i + 1) * P]
                    last = nc.vector.tensor_tensor_reduce(
                        out=sums, in0=sums, in1=ident[:], scale=1.0, scalar=0.0, op0=ALU.mult, op1=ALU.add,
                        accum_out=total[:, h * TH + i:h * TH + i + 1])
                last.then_inc(s_tot, 1)
                dve.wait_ge(s_tot, n * NH + h + 1)
                nc.vector.reciprocal(total_inv[:, tiles], total[:, tiles]).then_inc(s_ti, 1)

            def tile_out(n, i):
                dve.wait_ge(s_ti, n * NH + i // TH + 1)
                dve.wait_ge(s_res, n * NT + i + 1)
                dve.wait_ge(s_o, n * NT + i + 1)
                at = x_res[:, i % TH, :]
                nc.vector.scalar_tensor_tensor(out=at, in0=o_ps[i % 2], scalar=total_inv[:, i:i + 1],
                                               in1=at, op0=ALU.mult, op1=ALU.add).then_inc(s_y, 1)

            def setup_lo_parts(u0, hi, lo, first=0, end=KC):
                for k in range(first, end):
                    dve.wait_ge(s_seth, u0 + k + 1)
                    lo_part(lo[:, k, :], psum[:, (u0 + k) % SET_BANKS, :], hi[:, k, :], s_setr)

            vector_sums = [(w[:, k, :], vec[:], dst[:, k:k + 1]) for w, vec, dst in
                           ((w_k, bq_wide, wk_bq), (w_q, bk_wide, wq_bk)) for k in range(KC)]
            vector_sums.append((bq_wide[:], bk_wide[:], bqbk[:]))

            def sum_products(first, end):
                for n in range(first, end):
                    left, right, dst = vector_sums[n]
                    dve.wait_ge(s_setv, n + 1)
                    nc.vector.tensor_tensor_reduce(out=products[:], in0=left, in1=right, scale=1.0, scalar=0.0,
                                                   op0=ALU.mult, op1=ALU.add, accum_out=dst).then_inc(s_setv, 1)

            setup_lo_parts(SET_WQ, wq_t_hi, wq_t_lo)
            setup_lo_parts(SET_WK, wk_t_hi, wk_t_lo)
            dve.wait_ge(s_vec, 1)
            nc.vector.tensor_copy(vec_cols[:], vec_ps).then_inc(s_setv, 1)
            quarter_transpose(0, 0)
            quarter_transpose(0, 1)
            token_stats(0, 0, 0, KC)
            quarter_transpose(0, 2)
            quarter_transpose(0, 3)
            setup_lo_parts(SET_A, a_hi, a_lo, 0, 3)
            token_stats(0, 1, 0, KC)
            dve.wait_ge(s_sv, 1)
            channel_stats(0)
            setup_lo_parts(SET_A, a_hi, a_lo, 3, KC)
            setup_lo_parts(SET_WV, wv_t_hi, wv_t_lo, 0, 2)
            group_variance(0)
            setup_lo_parts(SET_WV, wv_t_hi, wv_t_lo, 2, KC)
            variance(0)
            dve.wait_ge(s_wide, 16 * 3)
            sum_products(0, 1)
            norm(0)
            xn_lo_parts(0)
            setup_lo_parts(SET_M, m_hi, m_lo, 0, 3)
            sum_products(1, KC)
            setup_lo_parts(SET_M, m_hi, m_lo, 3, KC)
            for j in range(KC):
                split_lo_part(0, "t", 0, j)
                sum_products(KC + 2 * j, min(KC + 2 * j + 2, 2 * KC + 1))
            dve.wait_ge(s_setv, SETV_VECTORS - 1)
            nc.vector.tensor_scalar(bqbk_part[:], bqbk[:], 1.0 / P, None, ALU.mult).then_inc(s_setv, 1)
            dve.wait_ge(s_setv, SETV_VECTORS)
            for k in range(KC):
                row_part(0, k)

            def image(b, more):
                def next_input(*after):
                    if more and after in TRANSPOSED:
                        quarter_transpose(b + 1, TRANSPOSED[after])
                    if more and after in MEASURED:
                        token_stats(b + 1, *MEASURED[after])

                split_lo_part(b, "v", 0, 0)
                split_lo_part(b, "v", 0, 1)
                next_input("v", 1)
                for m in range(NT):
                    top_part_step(b, 0, m)
                    next_input("s", m)
                for j in range(KC):
                    if more and j == KC - 1:
                        dve.wait_ge(s_sv, (b + 1) * STAT_STEPS + 1)
                    split_lo_part(b, "t", 1, j)
                    next_input("t", j)
                    if more and j == KC - 1:
                        channel_stats(b + 1)
                    if j == KC - 1:
                        tile_shift(b, 0)
                    shifts(b, 0, *SHIFTED.get(("t", j), (0, 0)))
                for m in range(2, NT):
                    split_lo_part(b, "v", 0, m)
                    shifts(b, 0, *SHIFTED.get(("v", m), (0, 0)))
                    pt_lo_parts(b, 0, *SPLIT_UP.get(("v", m), (0, 0)))
                    if more:
                        if m == 4:
                            group_variance(b + 1)
                for m in range(NT):
                    top_part_step(b, 1, m)
                    if more:
                        if m == 3:
                            variance(b + 1)
                        if m == 5:
                            norm(b + 1)
                totals(b, 0)
                if more:
                    xn_lo_parts(b + 1)
                tile_shift(b, 1)
                tile_out(b, 0)
                shifts(b, 1, 0, NT)
                if more:
                    for k in range(KC):
                        row_part(b + 1, k)
                        if k == 0:
                            tile_out(b, 1)
                for i in range(1 if not more else 2, TH):
                    tile_out(b, i)
                for j in range(KC):
                    pt_lo_parts(b, 1, 2 * j, 2 * j + 2)
                    if more:
                        split_lo_part(b + 1, "t", 0, j)
                totals(b, 1)
                for i in range(TH, NT):
                    tile_out(b, i)

            if B > 1:
                image(0, True)
            if B > 2:
                with dve.Fori(1, B - 1) as b:
                    image(b, True)
            image(B - 1, False)

        @block.tensor
        def _(pe):
            def product(dst, pairs, ready=()):
                for n, (s_hi_, s_lo_, m_hi_, m_lo_) in enumerate(pairs):
                    for signal, before in ready:
                        pe.wait_ge(signal, before + n + 1)
                    nc.tensor.matmul(dst, s_hi_, m_hi_, start=n == 0, stop=False)
                    nc.tensor.matmul(dst, s_hi_, m_lo_, start=False, stop=False)
                    last = nc.tensor.matmul(dst, s_lo_, m_hi_, start=False, stop=n == len(pairs) - 1)
                return last

            def chunk(c):
                return slice(c * P, (c + 1) * P)

            def setup_bank(u):
                if u >= SET_BANKS:
                    pe.wait_ge(s_setr, u - SET_BANKS + 1)
                return psum[:, u % SET_BANKS, :]

            def weight_transpose(u0, w, loaded):
                pe.wait_ge(loaded, 16 * NI)
                for j in range(KC):
                    bank = setup_bank(u0 + j)
                    for k in range(KC):
                        last = nc.tensor.transpose(bank[:, chunk(k)], w[:, k, chunk(j)], ident[:])
                    last.then_inc(s_set, 1)

            def weight_product(u0, left_hi, left_lo, right_hi, right_lo, ready, first=0, end=KC):
                for k in range(first, end):
                    product(setup_bank(u0 + k), [(left_hi[:, j, chunk(k)], left_lo[:, j, chunk(k)], right_hi[:, j, :],
                                                  right_lo[:, j, :]) for j in range(KC)],
                            ready if k == 0 else ()).then_inc(s_set, 1)

            def work_bank(n, *what):
                u = USES.index(what)
                last = USES[u - 4]
                before = 1 if u < 4 else 0
                if not (before and starts(n)):
                    if last[0] == "s":
                        pe.wait_ge(s_sr, n * SCORES + PLACE[last] + 1 - before * SCORES)
                    else:
                        pe.wait_ge(s_free, n * SPLIT + PLACE[last] + 1 - before * SPLIT)
                return bank_of(*what)

            def group_sum(n, step, rhs):
                pe.wait_ge(s_stin, n * 2 + step + 1)
                nc.tensor.matmul(stat[:, 0:KC], group_avg[:], rhs, start=True, stop=True).then_inc(s_stat, 1)

            def t_chunk(n, h, j):
                tokens = slice(h * BANK, (h + 1) * BANK)
                dst = work_bank(n, "t", h, j)
                product(dst, [(a_hi[:, k, chunk(j)], a_lo[:, k, chunk(j)], xn_hi[:, k, tokens], xn_lo[:, k, tokens])
                              for k in range(KC)], ((s_xl, n * KC),) if h == j == 0 else ()).then_inc(s_work, 1)

            def v_tile(n, m):
                dst = work_bank(n, "v", 0, m)
                product(dst, [(xn_hi[:, k, chunk(m)], xn_lo[:, k, chunk(m)], m_hi[:, k, :], m_lo[:, k, :])
                              for k in range(KC)]).then_inc(s_work, 1)

            def score_tile(n, h, m):
                if m == 0:
                    pe.wait_ge(s_free, n * SPLIT + PLACE[("t", h, KC - 1)] + 1)
                dst = work_bank(n, "s", h, m)
                product(dst, [(xn_hi[:, k, chunk(m)], xn_lo[:, k, chunk(m)], t_hi[:, k, :], t_lo[:, k, :])
                              for k in range(KC)]).then_inc(s_work, 1)

            def out_tile(n, i):
                h = i // TH
                if i == 0:
                    pe.wait_ge(s_free, (n + 1) * SPLIT)
                if i > 1 or not starts(n):
                    pe.wait_ge(s_y, n * NT + max(i - 1, 0))
                dst = o_ps[i % 2]
                for m in range(NT):
                    if i % TH == 0:
                        pe.wait_ge(s_ptl, (n * NH + h) * NT + m + 1)
                    queries = chunk(i % TH)
                    nc.tensor.matmul(dst, pt_hi[:, m, queries], v_hi[:, m, :], start=m == 0, stop=False)
                    nc.tensor.matmul(dst, pt_hi[:, m, queries], v_lo[:, m, :], start=False, stop=False)
                    last = nc.tensor.matmul(dst, pt_lo[:, m, queries], v_hi[:, m, :], start=False, stop=m == NT - 1)
                last.then_inc(s_o, 1)

            pe.wait_ge(s_const, 6)
            weight_transpose(SET_WQ, w_q, s_wload[0])
            weight_transpose(SET_WK, w_k, s_wload[1])
            pe.wait_ge(s_small, 16 * 3)
            nc.tensor.transpose(vec_ps, vec_rows[:], ident[0:3 * KC, 0:3 * KC]).then_inc(s_vec, 1)
            weight_product(SET_A, wq_t_hi, wq_t_lo, wk_t_hi, wk_t_lo, ((s_setr, SET_WK),))
            weight_transpose(SET_WV, w_v, s_wload[2])
            group_sum(0, 0, mv[:, :, 0])
            parts = (wv_t_hi, wv_t_lo, wp_hi, wp_lo, ((s_setr, SET_WV), (s_wpl, 0)))
            weight_product(SET_M, *parts, 0, 1)
            group_sum(0, 1, dev[:])
            weight_product(SET_M, *parts, 1, KC)
            for j in range(KC):
                pe.wait_ge(s_setr, max(u + 1 for u in range(SET_M + KC) if u % SET_BANKS == j))
                t_chunk(0, 0, j)
            pe.wait_ge(s_setr, SET_M + KC)

            def image(b, more):
                v_tile(b, 0)
                v_tile(b, 1)
                for m in range(NT):
                    score_tile(b, 0, m)
                for j in range(KC):
                    t_chunk(b, 1, j)
                for m in range(2, NT):
                    v_tile(b, m)
                    if more:
                        if m == 3:
                            group_sum(b + 1, 0, mv[:, :, 0])
                for m in range(NT):
                    score_tile(b, 1, m)
                    if more and m == 1:
                        group_sum(b + 1, 1, dev[:])
                for i in range(TH):
                    out_tile(b, i)
                if more:
                    for j in range(KC):
                        t_chunk(b + 1, 0, j)
                for i in range(TH, NT):
                    out_tile(b, i)

            if B > 1:
                image(0, True)
            if B > 2:
                with pe.Fori(1, B - 1) as b:
                    image(b, True)
            image(B - 1, False)


_INS = ["x"] + ["L0_conv_" + n for n in ("gamma", "beta", "wq", "bq", "wk", "bk", "wv", "bv", "wp", "bp")]


def kernel(**inputs):
    import numpy as _np
    import concourse.bacc as _bacc
    from concourse.bass_utils import run_bass_kernel_spmd as _run

    nc = _bacc.Bacc("TRN2", target_bir_lowering=False, num_devices=1)
    arrays, args = {}, []
    for name in _INS:
        a = _np.ascontiguousarray(inputs[name])
        arrays[f"in_{name}_dram"] = a
        args.append(nc.dram_tensor(f"in_{name}_dram", a.shape, mybir.dt.from_np(a.dtype), kind="ExternalInput").ap())
    args.append(nc.dram_tensor("out_dram", inputs["x"].shape, FP32, kind="ExternalOutput").ap())
    group_norm_attention(nc, *args)
    r = _run(nc, [arrays], core_ids=[0])
    return r.results[0]["out_dram"]
```
